# Optimizing a Trainium2 kernel written in Bass

```python
import numpy as np
import jax
import jax.numpy as jnp

def _softmax(x, axis=-1):
    return jax.nn.softmax(x, axis=axis)

def _gelu(x):
    return jax.nn.gelu(x, approximate=True)

def _silu(x):
    return jax.nn.silu(x)

def _sigmoid(x):
    return jax.nn.sigmoid(x)

def _layernorm(x, axis=-1, eps=1e-05):
    m = jnp.mean(x, axis=axis, keepdims=True)
    v = jnp.var(x, axis=axis, keepdims=True)
    return (x - m) / jnp.sqrt(v + eps)

def _scatter_add(tgt, idx, src, axis=0):
    return tgt.at[idx].add(src)

def _segment_sum(src, seg, n):
    return jax.ops.segment_sum(src, seg, n)
kernel_name = 'mk_adaln_d1_jaxref_r8_2d99ca'

def setup_inputs(seed: int=0):
    np.random.seed(seed)
    _w = jnp.asarray

    def _L0_attn_setup():
        import jax, jax.numpy as jnp
        import numpy as np
        B, S, D = (2, 256, 128)
        H = 16
        DK = 128
        DV = 128
        EPS = 1e-05
        key = jax.random.key(seed)
        k1, k2, k3, k4 = jax.random.split(key, 4)
        x = jax.random.normal(k1, (B, S, D), dtype=jnp.float32)
        Wq = jax.random.normal(k2, (DK, D), dtype=jnp.float32) * 0.02
        Wk = jax.random.normal(k3, (DK, D), dtype=jnp.float32) * 0.02
        Wv = jax.random.normal(k4, (DV, D), dtype=jnp.float32) * 0.02
        return {'x': x, 'Wq': Wq, 'Wk': Wk, 'Wv': Wv}
    _L0_attn_in = _L0_attn_setup()

    def _L0_ffn_setup():
        import jax, jax.numpy as jnp
        import numpy as np
        B, S, D, H, E, K = (2, 256, 128, 256, 8, 2)
        key = jax.random.key(seed)
        ks = jax.random.split(key, 8)
        s_in = 1.0 / np.sqrt(D)
        s_hid = 1.0 / np.sqrt(H)
        return {'x': jax.random.normal(ks[0], (B, S, D), dtype=jnp.float32), 'w1': jax.random.normal(ks[1], (E, D, H), dtype=jnp.float32) * s_in, 'b1': jax.random.normal(ks[2], (E, H), dtype=jnp.float32) * 0.01, 'w2': jax.random.normal(ks[3], (E, D, H), dtype=jnp.float32) * s_in, 'b2': jax.random.normal(ks[4], (E, H), dtype=jnp.float32) * 0.01, 'w3': jax.random.normal(ks[5], (E, H, D), dtype=jnp.float32) * s_hid, 'b3': jax.random.normal(ks[6], (E, D), dtype=jnp.float32) * 0.01, 'gate_w': jax.random.normal(ks[7], (D, E), dtype=jnp.float32) * s_in}
    _L0_ffn_in = _L0_ffn_setup()
    _L0_c = _w((lambda *s: np.random.randn(*s).astype(np.float32) * 0.05)(16, 128))
    _L0_wmod = _w((lambda *s: np.random.randn(*s).astype(np.float32) * 0.05)(128, 6 * 128) * 128 ** (-0.5))
    _d = {'L0_attn_x': _L0_attn_in['x'], 'L0_attn_Wq': _L0_attn_in['Wq'], 'L0_attn_Wk': _L0_attn_in['Wk'], 'L0_attn_Wv': _L0_attn_in['Wv'], 'L0_ffn_w1': _L0_ffn_in['w1'], 'L0_ffn_b1': _L0_ffn_in['b1'], 'L0_ffn_w2': _L0_ffn_in['w2'], 'L0_ffn_b2': _L0_ffn_in['b2'], 'L0_ffn_w3': _L0_ffn_in['w3'], 'L0_ffn_b3': _L0_ffn_in['b3'], 'L0_ffn_gate_w': _L0_ffn_in['gate_w'], 'L0_c': _L0_c, 'L0_wmod': _L0_wmod}
    _x0 = _d['L0_attn_x']
    _d['L0_attn_x'] = jax.random.normal(jax.random.fold_in(jax.random.key(seed), 1), (16, 512, 128), dtype=_x0.dtype)
    del _x0
    return _d

def reference(L0_attn_x, L0_attn_Wq, L0_attn_Wk, L0_attn_Wv, L0_ffn_w1, L0_ffn_b1, L0_ffn_w2, L0_ffn_b2, L0_ffn_w3, L0_ffn_b3, L0_ffn_gate_w, L0_c, L0_wmod):

    def _L0_attn_ref(x, Wq, Wk, Wv):
        import jax, jax.numpy as jnp
        import numpy as np
        B, S, D = (2, 256, 128)
        H = 16
        DK = 128
        DV = 128
        EPS = 1e-05
        b, s, d = x.shape
        dkh = DK // H
        dvh = DV // H
        Q = (x @ Wq.T).reshape(H, b, s, dkh)
        K = (x @ Wk.T).reshape(H, b, s, dkh)
        V = (x @ Wv.T).reshape(H, b, s, dvh)
        scores = jnp.einsum('hbqd,hbkd->hbqk', Q, K)
        atten = jax.nn.softmax(scores, axis=-1)
        out = jnp.einsum('hbqk,hbkd->hbqd', atten, V).reshape(b, s, -1)
        y = out + x
        mu = jnp.mean(y, axis=(1, 2), keepdims=True)
        var = jnp.var(y, axis=(1, 2), keepdims=True)
        return (y - mu) / jnp.sqrt(var + EPS)

    def _L0_ffn_ref(x, w1, b1, w2, b2, w3, b3, gate_w):
        import jax, jax.numpy as jnp
        import numpy as np
        B, S, D, H, E, K = (2, 256, 128, 256, 8, 2)
        logits = jnp.einsum('bsd,de->bse', x, gate_w)
        top_vals, top_idx = jax.lax.top_k(logits, K)
        gate_scores = jax.nn.softmax(top_vals, axis=-1)
        onehot = jax.nn.one_hot(top_idx, E, dtype=x.dtype)
        w_dense = jnp.einsum('bsk,bske->bse', gate_scores, onehot)
        h = jax.nn.silu(jnp.einsum('bsd,edh->ebsh', x, w1) + b1[:, None, None, :]) * (jnp.einsum('bsd,edh->ebsh', x, w2) + b2[:, None, None, :])
        expert_out = jnp.einsum('ebsh,ehd->ebsd', h, w3) + b3[:, None, None, :]
        return jnp.einsum('ebsd,bse->bsd', expert_out, w_dense)
    x = L0_attn_x
    mod = (_silu(L0_c) @ L0_wmod).reshape(L0_c.shape[0], 6, 1, -1)
    sa, ca, ga, sb, cb, gb = (mod[:, 0], mod[:, 1], mod[:, 2], mod[:, 3], mod[:, 4], mod[:, 5])
    ga = (2 * (ga >= 0) - 1) * jnp.maximum(jnp.abs(ga), 0.25)
    gb = (2 * (gb >= 0) - 1) * jnp.maximum(jnp.abs(gb), 0.25)
    h = _layernorm(x, axis=-1) * (1 + ca) + sa
    x = x + ga * _L0_attn_ref(h, L0_attn_Wq, L0_attn_Wk, L0_attn_Wv)
    h = _layernorm(x, axis=-1) * (1 + cb) + sb
    x = x + gb * _L0_ffn_ref(h, L0_ffn_w1, L0_ffn_b1, L0_ffn_w2, L0_ffn_b2, L0_ffn_w3, L0_ffn_b3, L0_ffn_gate_w)
    return x

_drawn_inputs = setup_inputs


def setup_inputs(seed=0):
    import zlib

    import numpy as np

    out = dict(_drawn_inputs(seed))
    spreads = {}
    factors = {'L0_attn_Wq': 8.0,
     'L0_attn_Wk': 8.0,
     'L0_attn_Wv': 8.0,
     'L0_ffn_b1': 50.381,
     'L0_ffn_b2': 53.035,
     'L0_ffn_b3': 30.673}
    for name, (base, spread) in spreads.items():
        noise = np.random.default_rng([zlib.crc32(name.encode()), seed]).standard_normal(out[name].shape)
        drawn = base * np.exp(spread * noise) if base else spread * noise
        out[name] = jnp.asarray(drawn.astype(out[name].dtype))
    for name, factor in factors.items():
        out[name] = (out[name] * factor).astype(out[name].dtype)
    return out
```

```python
from contextlib import ExitStack

import numpy as np
import concourse.bass as bass
from concourse import mybir

F32 = mybir.dt.float32
BF16 = mybir.dt.bfloat16
U32 = mybir.dt.uint32
I32 = mybir.dt.int32
ALU = mybir.AluOpType
ACT = mybir.ActivationFunctionType
AX_X = mybir.AxisListType.X

P = 128
NB, S, D = 16, 512, 128
HEADS, DK = 16, 8
G = D // DK
TOK = S // HEADS
PARTS = 3
ROWS = PARTS * PARTS * DK
MROW = 96
QUADS = 16
STEPS = 4 * QUADS
LAG = 8
TT = S // P
E, HID = 8, 256
HC = HID // P
EPS = 1e-5
DMA = 16


def misc_uses(b):
    uses = []
    if 1 <= b:
        uses.append((1, "max_rows", b - 1, 3))
    if 2 <= b:
        uses.append((2, "z_turn", b - 2, 0))
    if b + 1 < NB:
        uses += [(3, "x_turn", b + 1, 0), (4, "q", b + 1, 0)]
    if b < NB:
        uses.append((5, "max_rows", b, 0))
    if b + 1 < NB:
        uses += [(6, "k", b + 1, 0), (7, "v", b + 1, 0)]
    if b < NB:
        uses += [(9, "max_rows", b, 1), (13, "max_rows", b, 2)]
    if 1 <= b <= NB:
        uses += [(14, "mean", b - 1, 0), (15, "var", b - 1, 0)]
    return uses


def misc_table():
    order = [("x_turn", 0, 0), ("q", 0, 0), ("k", 0, 0), ("v", 0, 0)]
    for b in range(NB + 2):
        order += [u[1:] for u in misc_uses(b) if u[2] < NB]
    return {u: n for n, u in enumerate(order)}


MISC = misc_table()
MISC_PER_STAGE = len(misc_uses(5))


def misc_index(what, b, g=0):
    if isinstance(b, int):
        return MISC[(what, b, g)]
    return (b - 5) * MISC_PER_STAGE + MISC[(what, 5, g)]


def build(nc, x, wqT, wkT, wvT, w1, b1T, w2, b2T, w3, b3, gate_w, cT, wmod, out):
    ctx = ExitStack()
    with ctx:
        def sb(name, shape, dt=F32):
            return ctx.enter_context(nc.sbuf_tensor(name, shape, dt))

        def sem(name):
            return ctx.enter_context(nc.semaphore(name))

        def dram(name, shape, dt=F32):
            return nc.dram_tensor(name, shape, dt, kind="Internal").ap()

        q_dram = dram("q_dram", [PARTS, D, S], BF16)
        k_dram = dram("k_dram", [PARTS, D, S], BF16)
        v_dram = dram("v_dram", [S, D])
        h_dram = dram("h_dram", [NB, D, S])
        max_dram = dram("max_dram", [2, PARTS, 4, 4, P], BF16)
        o_dram = dram("o_dram", [2, 2, D, S])
        x2_dram = dram("x2_dram", [NB, S, D])
        gb_dram = dram("gb_dram", [NB, D])

        ident = sb("ident", [P, P])
        ident_bf = sb("ident_bf", [P, P], BF16)
        mean_mat = sb("mean_mat", [P, P])
        neg_half = sb("neg_half", [P, TT])
        iota8 = sb("iota8", [P, E])
        wq_sb = sb("wq_sb", [P, D])
        wk_sb = sb("wk_sb", [P, D])
        wv_sb = sb("wv_sb", [P, D])
        w1_sb = sb("w1_sb", [P, E, HID])
        w2_sb = sb("w2_sb", [P, E, HID])
        w3_sb = sb("w3_sb", [P, E, HC, D])
        b1_sb = sb("b1_sb", [P, HC, E])
        b2_sb = sb("b2_sb", [P, HC, E])
        b3_sb = sb("b3_sb", [P, TT, D])
        gw_sb = sb("gw_sb", [P, E])
        wmod_sb = sb("wmod_sb", [P, 6, D])
        c_sb = sb("c_sb", [P, NB])
        c_silu = sb("c_silu", [P, NB])
        mod = sb("mod", [P, 6, NB])
        mod_abs = sb("mod_abs", [P, 2, NB])
        mod_sign = sb("mod_sign", [P, 2, NB])
        gb_rows = sb("gb_rows", [NB, D])

        Qt = [sb(f"Qt{i}", [P, HEADS, S], BF16) for i in range(2)]
        Kt = [sb(f"Kt{i}", [P, HEADS, S], BF16) for i in range(2)]
        q_land = sb("q_land", [P, G, S], BF16)
        k_land = sb("k_land", [P, G, S], BF16)
        v_land = sb("v_land", [P, HEADS * 4, DK])
        Vt = sb("Vt", [P, 2, HEADS * 4, 2 * DK])
        probs = sb("probs", [P, 8, S])
        x_in = sb("x_in", [P, TT, D])
        x_stats = sb("x_stats", [P, TT, 6])
        x_mv = sb("x_mv", [P, TT, 2])
        x_ve = sb("x_ve", [P, TT])
        x_rstd = sb("x_rstd", [P, TT])
        x_shift = sb("x_shift", [P, TT])
        x_norm = sb("x_norm", [P, TT, D])
        hT = sb("hT", [P, S])
        q_f = sb("q_f", [P, S])
        k_f = sb("k_f", [P, S])
        v_f = sb("v_f", [P, TT, D])
        q_rest = sb("q_rest", [P, S])
        k_rest = sb("k_rest", [P, S])
        q_parts = sb("q_parts", [P, PARTS, S], BF16)
        k_parts = sb("k_parts", [P, PARTS, S], BF16)
        neg_max = sb("neg_max", [P, 2, 16])
        max_rest = sb("max_rest", [P, 16])
        max_parts = sb("max_parts", [P, PARTS, 16], BF16)
        max_rows = sb("max_rows", [PARTS * 16, P], BF16)
        o_sb = sb("o_sb", [P, 2, S])
        num_den = sb("num_den", [P, 2, S])
        h_back = sb("h_back", [P, S])
        x_back = sb("x_back", [P, TT, D])
        den_inv = sb("den_inv", [P, S])
        attn = sb("attn", [P, S])
        y = sb("y", [P, S])
        y_stats = sb("y_stats", [P, 6])
        y_mv = sb("y_mv", [P, 2])
        y_mean = sb("y_mean", [P, 1])
        y_dev = sb("y_dev", [P, 1])
        y_dev2 = sb("y_dev2", [P, 1])
        y_sq = sb("y_sq", [P, 1])
        y_ve = sb("y_ve", [P, 1])
        y_rstd = sb("y_rstd", [P, 1])
        y_scale = sb("y_scale", [P, 1])
        y_shift = sb("y_shift", [P, 1])
        z = sb("z", [P, S])
        x2_out = sb("x2_out", [P, TT, D])
        room_q = Qt[0][:].rearrange("p n q -> p (n q)").bitcast(F32)
        room_k = Kt[0][:].rearrange("p n q -> p (n q)").bitcast(F32)
        hidden = [room_q[:, i * S:(i + 1) * S] for i in range(4)]
        gate_act = room_q[:, 4 * S:6 * S].rearrange("p (c s) -> p c s", c=HC)
        acc = room_q[:, 6 * S:8 * S].rearrange("p (i t c) -> p i t c", i=2, t=TT)
        x2 = room_k[:, 0:2 * S].rearrange("p (i t c) -> p i t c", i=2, t=TT)
        y_out = room_k[:, 2 * S:4 * S].rearrange("p (i t c) -> p i t c", i=2, t=TT)
        h2T = [room_k[:, (4 + i) * S:(5 + i) * S] for i in range(2)]
        f_norm = room_k[:, 6 * S:7 * S].rearrange("p (t c) -> p t c", t=TT)
        gb_all = sb("gb_all", [P, 2, D])
        f_stats = sb("f_stats", [P, TT, 6])
        f_mv = sb("f_mv", [P, TT, 2])
        f_ve = sb("f_ve", [P, TT])
        f_rstd = sb("f_rstd", [P, TT])
        f_shift = sb("f_shift", [P, TT])
        logits = sb("logits", [P, TT, E])
        top = sb("top", [P, TT, 8])
        top_at = sb("top_at", [P, TT, 8], U32)
        top_at_f = sb("top_at_f", [P, TT, 2])
        top_gap = sb("top_gap", [P, TT])
        top_tanh = sb("top_tanh", [P, TT])
        score = sb("score", [P, 2, TT])
        pick = sb("pick", [P, 2, TT, E])
        w_dense = [sb(f"w_dense{i}", [P, TT, 32]) for i in range(2)]
        w_rows = [sb(f"w_rows{i}", [P, P]) for i in range(2)]

        bank = [ctx.enter_context(nc.psum_tensor(f"bank{i}", [P, S], F32)) for i in range(8)]
        score_a = bank[0:2]
        score_b = bank[2:6]
        pv_bank = bank[6]
        misc = bank[7]
        misc_bf = misc[:].bitcast(BF16)
        up_bank = bank[0:4]
        down_bank = bank[4:6]

        s_w = sem("s_w")
        s_expert_w = sem("s_expert_w")
        s_const = sem("s_const")
        s_clear = sem("s_clear")
        s_c_silu = sem("s_c_silu")
        s_mod_mm = sem("s_mod_mm")
        s_mod_chain = sem("s_mod_chain")
        s_mod = sem("s_mod")
        s_gb_mm = sem("s_gb_mm")
        s_gb = sem("s_gb")
        s_gb_dram = sem("s_gb_dram")
        s_misc_full = sem("s_misc_full")
        s_misc_read = sem("s_misc_read")
        s_x_in = sem("s_x_in")
        s_x_stats = sem("s_x_stats")
        s_x_mv = sem("s_x_mv")
        s_x_ve = sem("s_x_ve")
        s_x_rstd = sem("s_x_rstd")
        s_x_shift = sem("s_x_shift")
        s_x_norm = sem("s_x_norm")
        s_h_stored = sem("s_h_stored")
        s_split_q = [sem(f"s_split_q{i}") for i in range(4)]
        s_split_k = [sem(f"s_split_k{i}") for i in range(4)]
        s_q_stored = sem("s_q_stored")
        s_k_stored = sem("s_k_stored")
        s_v_stored = sem("s_v_stored")
        s_q_landed = sem("s_q_landed")
        s_k_landed = sem("s_k_landed")
        s_q_relaid = sem("s_q_relaid")
        s_k_relaid = sem("s_k_relaid")
        s_v_relaid = sem("s_v_relaid")
        s_v_loaded = sem("s_v_loaded")
        s_a = sem("s_a")
        s_max = sem("s_max")
        s_split_max = [sem(f"s_split_max{i}") for i in range(4)]
        s_max_stored = sem("s_max_stored")
        s_max_loaded = [sem(f"s_max_loaded{i}") for i in range(2)]
        s_b = sem("s_b")
        s_exp = sem("s_exp")
        s_pv = sem("s_pv")
        s_o = sem("s_o")
        s_o_stored = [sem(f"s_o_stored{i}") for i in range(2)]
        s_back = sem("s_back")
        s_den_inv = sem("s_den_inv")
        s_attn = sem("s_attn")
        s_y = sem("s_y")
        s_y_stats = sem("s_y_stats")
        s_y_mv = sem("s_y_mv")
        s_y_dev = sem("s_y_dev")
        s_y_dev2 = sem("s_y_dev2")
        s_y_sq = sem("s_y_sq")
        s_y_rstd = sem("s_y_rstd")
        s_y_scale = sem("s_y_scale")
        s_y_shift = sem("s_y_shift")
        s_z = sem("s_z")
        s_x2_stored = sem("s_x2_stored")
        s_x2 = [sem(f"s_x2_{i}") for i in range(2)]
        s_f_stats = sem("s_f_stats")
        s_f_mv = sem("s_f_mv")
        s_f_ve = sem("s_f_ve")
        s_f_rstd = sem("s_f_rstd")
        s_f_shift = sem("s_f_shift")
        s_f_norm = sem("s_f_norm")
        s_f_full = sem("s_f_full")
        s_f_read = sem("s_f_read")
        s_top = sem("s_top")
        s_top_at = sem("s_top_at")
        s_gap = sem("s_gap")
        s_tanh = sem("s_tanh")
        s_score = sem("s_score")
        s_pick = sem("s_pick")
        s_wd = sem("s_wd")
        s_up = sem("s_up")
        s_act = sem("s_act")
        s_hid = sem("s_hid")
        s_down = sem("s_down")
        s_acc = sem("s_acc")
        s_scaled = sem("s_scaled")
        s_fin = sem("s_fin")
        s_out = [sem(f"s_out{i}") for i in range(2)]

        block = ctx.enter_context(nc.Block())

        def over_stages(eng, stage):
            stage(0, 0)
            stage(1, 1)
            with eng.Fori(1, NB // 2 - 1, 1) as i:
                stage(2 * i, 0)
                stage(2 * i + 1, 1)
            for b in range(NB - 2, NB + 2):
                stage(b, b % 2)

        def has(b, first, last):
            return not isinstance(b, int) or first <= b <= last

        def later(b, n=1):
            return not isinstance(b, int) or b >= n

        N_CONST = 11

        def wait_apart(eng, semaphore, value):
            value = value if isinstance(value, int) else eng.to_reg(value)
            eng.wait_ge(s_const, N_CONST)
            eng.wait_ge(semaphore, value)

        @block.sync
        def _(sp):
            for dst, src in (
                (wmod_sb[:].rearrange("p j c -> p (j c)"), wmod), (c_sb[:], cT),
                (wq_sb[:], wqT), (wk_sb[:], wkT), (wv_sb[:], wvT), (gw_sb[:], gate_w),
            ):
                sp.dma_start(dst, src).then_inc(s_w, DMA)

            def x_load(b):
                if later(b):
                    wait_apart(sp, s_x_norm, b)
                sp.dma_start(x_in[:], x[b].rearrange("(t p) c -> p t c", p=P)).then_inc(s_x_in, DMA)

            def front_store(b, what):
                if what == "x_turn":
                    wait_apart(sp, s_misc_read, misc_index("x_turn", b) + 1)
                    sp.dma_start(h_dram[b], hT[:]).then_inc(s_h_stored, DMA)
                if what == "q":
                    sp.wait_ge(s_split_q[3], b + 1)
                    sp.dma_start(q_dram.rearrange("i c s -> c i s"), q_parts[:]).then_inc(s_q_stored, DMA)
                if what == "k":
                    sp.wait_ge(s_split_k[3], b + 1)
                    sp.dma_start(k_dram.rearrange("i c s -> c i s"), k_parts[:]).then_inc(s_k_stored, DMA)
                if what == "v":
                    sp.wait_ge(s_misc_read, misc_index("v", b) + 1)
                    sp.dma_start(v_dram.rearrange("(t p) c -> p t c", p=P), v_f[:]).then_inc(s_v_stored, DMA)

            def front_load(b, par):
                if later(b):
                    wait_apart(sp, s_q_relaid, b)
                sp.wait_ge(s_q_stored, (b + 1) * DMA)
                for i in range(PARTS):
                    for j in range(PARTS):
                        row = (PARTS * i + j) * DK
                        sp.dma_start(q_land[row:row + DK], q_dram[i].rearrange("(g d) s -> d g s", d=DK))\
                            .then_inc(s_q_landed, DMA)
                if later(b):
                    wait_apart(sp, s_k_relaid, b)
                sp.wait_ge(s_k_stored, (b + 1) * DMA)
                for i in range(PARTS):
                    for j in range(PARTS):
                        row = (PARTS * i + j) * DK
                        sp.dma_start(k_land[row:row + DK], k_dram[j].rearrange("(g d) s -> d g s", d=DK))\
                            .then_inc(s_k_landed, DMA)
                if later(b):
                    wait_apart(sp, s_v_relaid, b)
                sp.wait_ge(s_v_stored, (b + 1) * DMA)
                for g in range(4):
                    sp.dma_start(
                        v_land[32 * g:32 * g + TOK].rearrange("p (n i) d -> p n (i d)", n=HEADS),
                        v_dram.rearrange("(n p) (g w) -> g p n w", p=TOK, g=4)[g]).then_inc(s_v_loaded, DMA)

            def max_move(b, par, g):
                gg = 4 * b + g
                sp.wait_ge(s_misc_read, misc_index("max_rows", b, g) + 1)
                sp.dma_start(max_dram[g % 2].rearrange("i h c p -> (i h c) p"), max_rows[:])\
                    .then_inc(s_max_stored, DMA)
                sp.wait_ge(s_max_stored, (gg + 1) * DMA)
                sp.dma_start(Qt[par][MROW:MROW + PARTS, 4 * g:4 * g + 4],
                             max_dram[g % 2].rearrange("i h c p -> i h (c p)")).then_inc(s_max_loaded[g % 2], DMA)

            def o_store(b, par, g):
                sp.wait_ge(s_o, 4 * b + g + 1)
                for h in range(4):
                    for w in range(2):
                        sp.dma_start(
                            o_dram[par, w, :, P * g + TOK * h:P * g + TOK * h + TOK]
                            .rearrange("(g d) s -> d g s", d=DK),
                            o_sb[32 * h + DK * w:32 * h + DK * w + DK, g % 2, :]
                            .rearrange("d (g s) -> d g s", s=TOK)).then_inc(s_o_stored[g % 2], DMA)

            def back_load(b, par):
                for i in range(2):
                    sp.wait_ge(s_o_stored[i], (b + 1) * 16 * DMA)
                if later(b):
                    sp.wait_ge(s_y, b)
                    sp.wait_ge(s_misc_read, misc_index("z_turn", b - 1) + 1)
                sp.dma_start(num_den[:], o_dram[par].rearrange("w c s -> c w s")).then_inc(s_back, DMA)
                wait_apart(sp, s_h_stored, (b + 1) * DMA)
                sp.dma_start(h_back[:], h_dram[b]).then_inc(s_back, DMA)
                sp.dma_start(x_back[:], x[b].rearrange("(t p) c -> p t c", p=P)).then_inc(s_back, DMA)

            def x2_store(b):
                wait_apart(sp, s_misc_read, misc_index("z_turn", b) + 1)
                sp.dma_start(x2_dram[b].rearrange("(t p) c -> p t c", p=P), x2_out[:]).then_inc(s_x2_stored, DMA)

            def stage(b, par):
                if has(b, 0, NB - 2):
                    x_load(b + 1)
                if has(b, 1, NB):
                    o_store(b - 1, 1 - par, 1)
                    max_move(b - 1, 1 - par, 3)
                if has(b, 2, NB + 1):
                    x2_store(b - 2)
                if has(b, 0, NB - 2):
                    front_store(b + 1, "x_turn")
                if has(b, 1, NB):
                    o_store(b - 1, 1 - par, 2)
                if has(b, 0, NB - 1):
                    max_move(b, par, 0)
                if has(b, 0, NB - 2):
                    for what in ("q", "v", "k"):
                        front_store(b + 1, what)
                if has(b, 1, NB):
                    o_store(b - 1, 1 - par, 3)
                if has(b, 0, NB - 1):
                    max_move(b, par, 1)
                if has(b, 1, NB):
                    back_load(b - 1, 1 - par)
                if has(b, 0, NB - 2):
                    front_load(b + 1, 1 - par)
                if has(b, 0, NB - 1):
                    o_store(b, par, 0)
                    max_move(b, par, 2)

            x_load(0)
            for dst, src in (
                (w1_sb[:], w1.rearrange("e i h -> i e h")), (w2_sb[:], w2.rearrange("e i h -> i e h")),
                (b1_sb[:], b1T.rearrange("(c p) e -> p c e", p=P)),
                (b2_sb[:], b2T.rearrange("(c p) e -> p c e", p=P)),
            ):
                sp.dma_start(dst, src).then_inc(s_expert_w, DMA)
            for c in range(HC):
                sp.dma_start(w3_sb[:, :, c], w3[:, c * P:(c + 1) * P].rearrange("e p d -> p e d")).then_inc(s_expert_w, DMA)
            sp.wait_ge(s_const, N_CONST)
            for t in range(TT):
                sp.dma_start(b3_sb[32 * t:32 * t + E, t], b3).then_inc(s_expert_w, DMA)
            for what in ("x_turn", "q", "k", "v"):
                front_store(0, what)
            sp.wait_ge(s_clear, 4)
            front_load(0, 0)
            over_stages(sp, stage)

            def f_load(b, par):
                if later(b, 2):
                    wait_apart(sp, s_fin, b - 1)
                sp.dma_start(x2[:, par], x2_dram[b].rearrange("(t p) c -> p t c", p=P)).then_inc(s_x2[par], DMA)
                sp.dma_start(gb_all[:, par], gb_dram[bass.ds(b, 1)].broadcast_to([P, D])).then_inc(s_x2[par], DMA)

            def f_store(b, par):
                wait_apart(sp, s_fin, b + 1)
                sp.dma_start(out[b].rearrange("(t p) c -> p t c", p=P), y_out[:, par]).then_inc(s_out[par], DMA)

            sp.wait_ge(s_gb, 1)
            sp.dma_start(gb_dram, gb_rows[:]).then_inc(s_gb_dram, DMA)
            sp.wait_ge(s_gb_dram, DMA)
            sp.wait_ge(s_x2_stored, NB * DMA)
            f_load(0, 0)
            f_load(1, 1)
            with sp.Fori(0, NB // 2 - 1, 1) as i:
                for par in range(2):
                    f_store(2 * i + par, par)
                    f_load(2 * i + par + 2, par)
            for b in (NB - 2, NB - 1):
                f_store(b, b % 2)
            for par in range(2):
                sp.wait_ge(s_out[par], NB // 2 * DMA)

        @block.gpsimd
        def _(pool):
            pool.memset(ident[:], 0.0).then_inc(s_const, 1)
            pool.memset(ident_bf[:], 0.0).then_inc(s_const, 1)
            pool.memset(mean_mat[:], 1.0 / P).then_inc(s_const, 1)
            pool.memset(neg_half[:], -0.5).then_inc(s_const, 1)
            pool.iota(iota8[:], [[1, E]], base=0, channel_multiplier=0,
                      allow_small_or_imprecise_dtypes=True).then_inc(s_const, 1)
            pool.memset(Vt[:], 1.0).then_inc(s_const, 1)
            pool.memset(b3_sb[:], 0.0).then_inc(s_const, 1)
            pool.wait_ge(s_const, 7)
            for m in (ident, ident_bf):
                pool.affine_select(out=m[:], in_=m[:], compare_op=ALU.not_equal, fill=1.0, base=0,
                                   pattern=[[-1, P]], channel_multiplier=1).then_inc(s_const, 1)
            for i in range(2):
                pool.memset(w_dense[i][:], 0.0).then_inc(s_const, 1)

            def split(src, rest, parts, done, k):
                pool.tensor_copy(parts[:, 0], src).then_inc(done[0], 1)
                pool.wait_ge(done[0], k + 1)
                pool.tensor_tensor(rest, src, parts[:, 0], ALU.subtract).then_inc(done[1], 1)
                wait_apart(pool, done[1], k + 1)
                pool.tensor_copy(parts[:, 1], rest).then_inc(done[2], 1)
                pool.wait_ge(done[2], k + 1)
                pool.tensor_tensor(parts[:, 2], rest, parts[:, 1], ALU.subtract).then_inc(done[3], 1)

            def split_q(b):
                wait_apart(pool, s_misc_read, misc_index("q", b) + 1)
                if later(b):
                    wait_apart(pool, s_q_stored, b * DMA)
                split(q_f[:], q_rest[:], q_parts, s_split_q, b)

            def split_k(b):
                wait_apart(pool, s_misc_read, misc_index("k", b) + 1)
                if later(b):
                    wait_apart(pool, s_k_stored, b * DMA)
                split(k_f[:], k_rest[:], k_parts, s_split_k, b)

            def split_max(b, g):
                gg = 4 * b + g
                pool.wait_ge(s_max, (gg + 1) * 16)
                if g or later(b):
                    pb, pg = (b, g - 1) if g else (b - 1, 3)
                    wait_apart(pool, s_misc_full, misc_index("max_rows", pb, pg) + 1)
                split(neg_max[:, g % 2], max_rest[:], max_parts, s_split_max, gg)

            def relay(b, par, land, dst, landed, done):
                wait_apart(pool, landed, (b + 1) * PARTS * PARTS * DMA)
                if later(b, 2):
                    wait_apart(pool, s_b, (b - 1) * STEPS)
                pool.tensor_copy(
                    dst[par][:].rearrange("p n q -> p (n q)").bitcast(I32)
                    .rearrange("p (n g s) -> p n g s", n=HEADS, g=G),
                    land[:].rearrange("p g s -> p (g s)").bitcast(I32)
                    .rearrange("p (g n s) -> p n g s", n=HEADS, g=G)).then_inc(done, 1)

            def relay_v(b, par):
                wait_apart(pool, s_v_loaded, (b + 1) * 4 * DMA)
                if later(b, 2):
                    wait_apart(pool, s_pv, (b - 1) * QUADS)
                pool.tensor_copy(Vt[:, par, :, 0:DK], v_land[:]).then_inc(s_v_relaid, 1)

            def x_power(b):
                pool.wait_ge(s_x_ve, b + 1)
                pool.tensor_tensor(x_rstd[:], x_ve[:], neg_half[:], ALU.pow).then_inc(s_x_rstd, 1)

            def y_power(b):
                pool.wait_ge(s_misc_read, misc_index("var", b) + 1)
                pool.tensor_tensor(y_rstd[:], y_ve[:], neg_half[:, 0:1], ALU.pow).then_inc(s_y_rstd, 1)

            def add_h(b):
                pool.wait_ge(s_den_inv, b + 1)
                pool.tensor_tensor(attn[:], num_den[:, 0], den_inv[:], ALU.mult).then_inc(s_attn, 1)
                pool.wait_ge(s_attn, b + 1)
                if later(b):
                    pool.wait_ge(s_z, b)
                pool.tensor_tensor(y[:], attn[:], h_back[:], ALU.add).then_inc(s_y, 1)

            def stage(b, par):
                if has(b, 2, NB + 1):
                    y_power(b - 2)
                if has(b, 1, NB):
                    split_max(b - 1, 3)
                if has(b, 0, NB - 2):
                    x_power(b + 1)
                if has(b, 0, NB - 1):
                    split_max(b, 0)
                if has(b, 0, NB - 2):
                    split_q(b + 1)
                    split_k(b + 1)
                if has(b, 0, NB - 1):
                    split_max(b, 1)
                if has(b, 0, NB - 2):
                    relay(b + 1, 1 - par, q_land, Qt, s_q_landed, s_q_relaid)
                if has(b, 1, NB):
                    add_h(b - 1)
                if has(b, 0, NB - 1):
                    split_max(b, 2)
                if has(b, 0, NB - 2):
                    relay(b + 1, 1 - par, k_land, Kt, s_k_landed, s_k_relaid)
                    relay_v(b + 1, 1 - par)

            x_power(0)
            split_q(0)
            split_k(0)
            relay(0, 0, q_land, Qt, s_q_landed, s_q_relaid)
            relay(0, 0, k_land, Kt, s_k_landed, s_k_relaid)
            relay_v(0, 0)
            over_stages(pool, stage)

            with pool.Fori(0, NB, 1) as b:
                pool.wait_ge(s_f_ve, b + 1)
                pool.tensor_tensor(f_rstd[:], f_ve[:], neg_half[:], ALU.pow).then_inc(s_f_rstd, 1)

        @block.vector
        def _(dve):
            for t in (q_land, k_land):
                dve.memset(t[:].rearrange("p g s -> p (g s)").bitcast(I32), 0).then_inc(s_clear, 1)
            dve.memset(pv_bank[:], 0.0).then_inc(s_clear, 1)
            dve.wait_ge(s_clear, 2)
            dve.memset(k_land[MROW:MROW + PARTS], 1.0).then_inc(s_clear, 1)

            link_count = [0]

            def link(ins):
                link_count[0] += 1
                ins.then_inc(s_mod_chain, 1)
                dve.wait_ge(s_mod_chain, link_count[0])

            dve.wait_ge(s_mod_mm, 1)
            link(dve.tensor_copy(mod[:].rearrange("p j b -> p (j b)"), misc[:, 0:6 * NB]))
            gates = mod[:].rearrange("p (k j) b -> p k j b", j=3)[:, :, 2]
            scales = mod[:].rearrange("p (k j) b -> p k j b", j=3)[:, :, 1]
            link(dve.tensor_scalar(scales, scales, 1.0, None, ALU.add))
            link(dve.tensor_scalar(mod_sign[:], gates, 0.0, 2.0, ALU.is_ge, ALU.mult))
            link(dve.tensor_scalar(mod_sign[:], mod_sign[:], 1.0, None, ALU.subtract))
            link(dve.tensor_tensor(mod_abs[:], mod_sign[:], gates, ALU.mult))
            link(dve.tensor_scalar(mod_abs[:], mod_abs[:], 0.25, None, ALU.max))
            dve.tensor_tensor(gates, mod_sign[:], mod_abs[:], ALU.mult).then_inc(s_mod, 1)
            dve.wait_ge(s_gb_mm, 1)
            dve.tensor_copy(gb_rows[:], misc[0:NB, 0:D]).then_inc(s_gb, 1)

            def stats(src, st, mv, ve, k, s_st, s_mv, s_ve):
                for t in range(TT):
                    dve.bn_stats(st[:, t], src[:, t]).then_inc(s_st, 1)
                wait_apart(dve, s_st, TT * (k + 1))
                for t in range(TT):
                    dve.bn_aggr(mv[:, t], st[:, t]).then_inc(s_mv, 1)
                dve.wait_ge(s_mv, TT * (k + 1))
                dve.tensor_scalar(ve[:], mv[:, :, 1], EPS, None, ALU.add).then_inc(s_ve, 1)

            def normalise(src, dst, mv, rs, shift, k, s_shift, done):
                dve.scalar_tensor_tensor(shift[:], mv[:, :, 0], -1.0, rs[:], ALU.mult, ALU.mult)\
                    .then_inc(s_shift, 1)
                dve.wait_ge(s_shift, k + 1)
                for t in range(TT):
                    ins = dve.tensor_scalar(dst[:, t], src[:, t], rs[:, t:t + 1], shift[:, t:t + 1],
                                            ALU.mult, ALU.add)
                ins.then_inc(done, 1)

            def front_stats(b):
                dve.wait_ge(s_x_in, (b + 1) * DMA)
                stats(x_in, x_stats, x_mv, x_ve, b, s_x_stats, s_x_mv, s_x_ve)

            def front_norm(b):
                dve.wait_ge(s_x_rstd, b + 1)
                if later(b):
                    dve.wait_ge(s_misc_full, misc_index("x_turn", b - 1) + 1)
                normalise(x_in, x_norm, x_mv, x_rstd, x_shift, b, s_x_shift, s_x_norm)

            def maxima(b, r):
                g, c = r // 4, r % 4
                if c == 0 and (g >= 2 or later(b)):
                    dve.wait_ge(s_split_max[3], 4 * b + g - 1)
                for h in range(4):
                    dve.wait_ge(s_a, b * STEPS + 4 * r + h + 1)
                    dve.tensor_reduce(neg_max[:, g % 2, 4 * h + c:4 * h + c + 1], score_a[h % 2][:],
                                      AX_X, ALU.max, negate=True).then_inc(s_max, 1)

            def end_inv(b):
                dve.wait_ge(s_back, (b + 1) * 3 * DMA)
                dve.reciprocal(den_inv[:], num_den[:, 1]).then_inc(s_den_inv, 1)

            def end_stats(b):
                dve.wait_ge(s_y, b + 1)
                dve.bn_stats(y_stats[:], y[:]).then_inc(s_y_stats, 1)
                wait_apart(dve, s_y_stats, b + 1)
                dve.bn_aggr(y_mv[:], y_stats[:]).then_inc(s_y_mv, 1)

            def end_dev(b):
                dve.wait_ge(s_misc_full, misc_index("mean", b) + 1)
                dve.tensor_copy(y_mean[:], misc[:, 0:1]).then_inc(s_misc_read, 1)
                dve.wait_ge(s_misc_read, misc_index("mean", b) + 1)
                dve.tensor_tensor(y_dev[:], y_mv[:, 0:1], y_mean[:], ALU.subtract).then_inc(s_y_dev, 1)
                dve.wait_ge(s_y_dev, b + 1)
                dve.tensor_tensor(y_dev2[:], y_dev[:], y_dev[:], ALU.mult).then_inc(s_y_dev2, 1)
                dve.wait_ge(s_y_dev2, b + 1)
                dve.tensor_tensor(y_sq[:], y_dev2[:], y_mv[:, 1:2], ALU.add).then_inc(s_y_sq, 1)

            def end_var(b):
                dve.wait_ge(s_misc_full, misc_index("var", b) + 1)
                dve.tensor_scalar(y_ve[:], misc[:, 0:1], EPS, None, ALU.add).then_inc(s_misc_read, 1)

            def end_z(b):
                dve.wait_ge(s_y_rstd, b + 1)
                dve.tensor_tensor(y_scale[:], mod[:, 2, bass.ds(b, 1)], y_rstd[:], ALU.mult).then_inc(s_y_scale, 1)
                dve.wait_ge(s_y_scale, b + 1)
                dve.scalar_tensor_tensor(y_shift[:], y_mean[:], -1.0, y_scale[:], ALU.mult, ALU.mult)\
                    .then_inc(s_y_shift, 1)
                dve.wait_ge(s_y_shift, b + 1)
                if later(b):
                    dve.wait_ge(s_misc_full, misc_index("z_turn", b - 1) + 1)
                dve.tensor_scalar(z[:], y[:], y_scale[:], y_shift[:], ALU.mult, ALU.add).then_inc(s_z, 1)

            def end_x2(b):
                dve.wait_ge(s_misc_full, misc_index("z_turn", b) + 1)
                if later(b):
                    dve.wait_ge(s_x2_stored, b * DMA)
                dve.tensor_tensor(x2_out[:].rearrange("p t c -> p (t c)"), misc[:],
                                  x_back[:].rearrange("p t c -> p (t c)"), ALU.add).then_inc(s_misc_read, 1)

            def stage(b, par):
                for r in range(QUADS):
                    if has(b, 0, NB - 1):
                        maxima(b, r)
                    if r == 0 and has(b, 0, NB - 2):
                        front_stats(b + 1)
                    if r == 1 and has(b, 2, NB + 1):
                        end_z(b - 2)
                    if r == 1 and has(b, 0, NB - 2):
                        front_norm(b + 1)
                    if r == 2 and has(b, 2, NB + 1):
                        end_x2(b - 2)
                    if r == 11 and has(b, 1, NB):
                        end_inv(b - 1)
                    if r == 13 and has(b, 1, NB):
                        end_stats(b - 1)
                    if r == 14 and has(b, 1, NB):
                        end_dev(b - 1)
                    if r == 15 and has(b, 1, NB):
                        end_var(b - 1)

            front_stats(0)
            front_norm(0)
            over_stages(dve, stage)

            def f_piece(b, par, e):
                if e == 0:
                    dve.wait_ge(s_x2[par], (b - par + 2) * DMA)
                    stats(x2[:, par], f_stats, f_mv, f_ve, b, s_f_stats, s_f_mv, s_f_ve)
                if e == 1:
                    dve.wait_ge(s_f_rstd, b + 1)
                    if later(b):
                        dve.wait_ge(s_f_full, 4 * b - 3)
                    normalise(x2[:, par], f_norm, f_mv, f_rstd, f_shift, b, s_f_shift, s_f_norm)
                if e == 3:
                    dve.wait_ge(s_f_full, 4 * b + 2)
                    dve.tensor_copy(logits[:].rearrange("p t e -> p (t e)"), misc[:, 0:TT * E])\
                        .then_inc(s_f_read, 1)
                    wait_apart(dve, s_f_read, 4 * b + 2)
                    for t in range(TT):
                        dve.max(top[:, t], logits[:, t]).then_inc(s_top, 1)
                    dve.wait_ge(s_top, TT * (b + 1))
                    if later(b):
                        dve.wait_ge(s_tanh, b)
                    dve.tensor_tensor(top_gap[:], top[:, :, 0], top[:, :, 1], ALU.subtract).then_inc(s_gap, 1)
                    for t in range(TT):
                        dve.max_index(top_at[:, t], top[:, t], logits[:, t]).then_inc(s_top_at, 1)
                if e == 4:
                    dve.wait_ge(s_top_at, (TT + 1) * b + TT)
                    dve.tensor_copy(top_at_f[:], top_at[:, :, 0:2]).then_inc(s_top_at, 1)
                    dve.wait_ge(s_tanh, b + 1)
                    for k in range(2):
                        dve.tensor_scalar(score[:, k], top_tanh[:], 0.5 - k, 0.5, ALU.mult, ALU.add)\
                            .then_inc(s_score, 1)
                    dve.wait_ge(s_top_at, (TT + 1) * (b + 1))
                    dve.wait_ge(s_score, 2 * (b + 1))
                    for k in range(2):
                        for t in range(TT):
                            dve.tensor_scalar(pick[:, k, t], iota8[:], top_at_f[:, t, k:k + 1],
                                              score[:, k, t:t + 1], ALU.is_equal, ALU.mult).then_inc(s_pick, 1)
                    dve.wait_ge(s_pick, 2 * TT * (b + 1))
                    dve.tensor_tensor(w_dense[par][:, :, 0:E], pick[:, 0], pick[:, 1], ALU.add).then_inc(s_wd, 1)
                if e == 6:
                    dve.wait_ge(s_f_full, 4 * b + 4)
                    dve.tensor_copy(acc[:, par].rearrange("p t c -> p (t c)"), misc[:]).then_inc(s_f_read, 1)

            def expert(b, par, e):
                for c in range(HC):
                    u = (b * E + e) * HC + c
                    slot = HC * (e % 2) + c
                    dve.wait_ge(s_act, u + 1)
                    if e >= 2 or later(b):
                        dve.wait_ge(s_down, b * E + e - 1)
                    dve.scalar_tensor_tensor(hidden[slot], up_bank[2 * c + 1][:], b2_sb[:, c, e:e + 1],
                                             gate_act[:, c], ALU.add, ALU.mult).then_inc(s_hid, 1)

            def add_expert(b, par, e):
                w = b * E + e
                dve.wait_ge(s_down, w + 1)
                if e or later(b):
                    dve.wait_ge(s_acc, w)
                if e == 0:
                    dve.wait_ge(s_f_read, 4 * b + 4)
                for t in range(TT):
                    ins = dve.scalar_tensor_tensor(acc[:, par, t], down_bank[e % 2][:, P * t:P * t + P],
                                                   w_dense[par][:, t, e:e + 1], acc[:, par, t],
                                                   ALU.mult, ALU.add)
                ins.then_inc(s_acc, 1)

            def finish(b, par):
                dve.wait_ge(s_acc, (b + 1) * E)
                if later(b, 2):
                    dve.wait_ge(s_out[par], (b - par) * (DMA // 2))
                dve.tensor_tensor(y_out[:, par], acc[:, par],
                                  gb_all[:, par].unsqueeze(1).broadcast_to([P, TT, D]), ALU.mult)\
                    .then_inc(s_scaled, 1)
                dve.wait_ge(s_scaled, b + 1)
                dve.tensor_tensor(y_out[:, par], y_out[:, par], x2[:, par], ALU.add).then_inc(s_fin, 1)

            def f_batch(b, par, ahead):
                for e in range(E):
                    expert(b, par, e)
                    if e:
                        add_expert(b, par, e - 1)
                    if ahead:
                        f_piece(b + 1, 1 - par, e)
                add_expert(b, par, E - 1)
                finish(b, par)

            for e in range(E):
                f_piece(0, 0, e)
            f_batch(0, 0, True)
            f_batch(1, 1, True)
            with dve.Fori(1, NB // 2 - 1, 1) as i:
                f_batch(2 * i, 0, True)
                f_batch(2 * i + 1, 1, True)
            f_batch(NB - 2, 0, True)
            f_batch(NB - 1, 1, False)

        @block.scalar
        def _(act):
            act.wait_ge(s_w, 6 * DMA)
            act.activation(c_silu[:], c_sb[:], ACT.Silu).then_inc(s_c_silu, 1)
            act.wait_ge(s_mod, 1)

            def evacuate(what, b, g=0):
                act.wait_ge(s_misc_full, misc_index(what, b, g) + 1)
                if what == "x_turn":
                    if later(b):
                        act.wait_ge(s_h_stored, b * DMA)
                    ins = act.activation(hT[:], misc[:], ACT.Identity, bias=mod[:, 0, bass.ds(b, 1)],
                                         scale=mod[:, 1, bass.ds(b, 1)])
                if what == "q":
                    if later(b):
                        act.wait_ge(s_split_q[1], b)
                    ins = act.activation(q_f[:], misc[:], ACT.Copy)
                if what == "k":
                    if later(b):
                        act.wait_ge(s_split_k[1], b)
                    ins = act.activation(k_f[:], misc[:], ACT.Copy)
                if what == "v":
                    if later(b):
                        act.wait_ge(s_v_stored, b * DMA)
                    ins = act.activation(v_f[:].rearrange("p t c -> p (t c)"), misc[:], ACT.Copy)
                if what == "max_rows":
                    if g or later(b):
                        act.wait_ge(s_max_stored, (4 * b + g) * DMA)
                    ins = act.activation(max_rows[:], misc_bf[0:PARTS * 16, 0:P], ACT.Copy)
                ins.then_inc(s_misc_read, 1)

            def exps(b, j):
                if j >= 2 or later(b):
                    act.wait_ge(s_pv, b * QUADS + j - 1)
                for h in range(4):
                    n = b * STEPS + 4 * j + h
                    act.wait_ge(s_b, n + 1)
                    act.activation(probs[:, 4 * (j % 2) + h], score_b[h][:], ACT.Exp).then_inc(s_exp, 1)

            def copy_o(b, g):
                act.wait_ge(s_pv, b * QUADS + 4 * g + 4)
                if g >= 2 or later(b):
                    act.wait_ge(s_o_stored[g % 2], (2 * b + g // 2) * 8 * DMA)
                act.activation(o_sb[:, g % 2], pv_bank[:], ACT.Copy).then_inc(s_o, 1)

            def stage(b, par):
                for r in range(QUADS):
                    if r < LAG and has(b, 1, NB):
                        exps(b - 1, r + LAG)
                    if r >= LAG and has(b, 0, NB - 1):
                        exps(b, r - LAG)
                    if r in (0, 4, 8) and has(b, 1, NB):
                        copy_o(b - 1, 1 + r // 4)
                    if r == 12 and has(b, 0, NB - 1):
                        copy_o(b, 0)
                    for q, what, db, g in misc_uses(5):
                        if q == r and what in ("x_turn", "q", "k", "v", "max_rows"):
                            if has(b, max(0, 5 - db), NB - 1 + 5 - db):
                                evacuate(what, b + (db - 5), g)

            for what in ("x_turn", "q", "k", "v"):
                evacuate(what, 0)
            over_stages(act, stage)

            def f_piece(b, par, e):
                if e == 2:
                    act.wait_ge(s_f_full, 4 * b + 1)
                    act.activation(h2T[par], misc[:], ACT.Identity, bias=mod[:, 3, bass.ds(b, 1)],
                                   scale=mod[:, 4, bass.ds(b, 1)]).then_inc(s_f_read, 1)
                if e == 4:
                    act.wait_ge(s_gap, b + 1)
                    if later(b):
                        act.wait_ge(s_score, 2 * b)
                    act.activation(top_tanh[:], top_gap[:], ACT.Tanh, scale=0.5).then_inc(s_tanh, 1)
                if e == 5:
                    act.wait_ge(s_f_full, 4 * b + 3)
                    act.activation(w_rows[par][:], misc[:, 0:P], ACT.Copy).then_inc(s_f_read, 1)

            def expert(b, par, e):
                for c in range(HC):
                    u = (b * E + e) * HC + c
                    act.wait_ge(s_up, u + 1)
                    if e or later(b):
                        act.wait_ge(s_hid, u - 1)
                    act.activation(gate_act[:, c], up_bank[2 * c][:], ACT.Silu, bias=b1_sb[:, c, e:e + 1])\
                        .then_inc(s_act, 1)

            def f_batch(b, par, ahead):
                for e in range(E):
                    expert(b, par, e)
                    if ahead:
                        f_piece(b + 1, 1 - par, e)

            for e in range(E):
                f_piece(0, 0, e)
            f_batch(0, 0, True)
            f_batch(1, 1, True)
            with act.Fori(1, NB // 2 - 1, 1) as i:
                f_batch(2 * i, 0, True)
                f_batch(2 * i + 1, 1, True)
            f_batch(NB - 2, 0, True)
            f_batch(NB - 1, 1, False)

        @block.tensor
        def _(pe):
            pe.wait_ge(s_w, 6 * DMA)
            pe.wait_ge(s_const, N_CONST)
            pe.wait_ge(s_c_silu, 1)
            for j in range(6):
                ins = pe.matmul(misc[:, j * NB:(j + 1) * NB], wmod_sb[:, j], c_silu[:], start=True, stop=True)
            ins.then_inc(s_mod_mm, 1)
            pe.wait_ge(s_mod, 1)
            pe.transpose(misc[0:NB, 0:D], mod[:, 5], ident[:]).then_inc(s_gb_mm, 1)
            pe.wait_ge(s_gb, 1)

            def fill(what, b, g=0):
                n = misc_index(what, b, g)
                if what != "x_turn" or later(b):
                    pe.wait_ge(s_misc_read, n)
                if what == "x_turn":
                    pe.wait_ge(s_x_norm, b + 1)
                    for t in range(TT):
                        ins = pe.transpose(misc[:, P * t:P * t + P], x_norm[:, t], ident[:])
                if what in ("q", "k"):
                    w = wq_sb if what == "q" else wk_sb
                    ins = pe.matmul(misc[:], w[:], hT[:], start=True, stop=True)
                if what == "v":
                    for t in range(TT):
                        ins = pe.matmul(misc[:, P * t:P * t + P], hT[:, P * t:P * t + P], wv_sb[:],
                                        start=True, stop=True)
                if what == "max_rows":
                    wait_apart(pe, s_split_max[3], 4 * b + g + 1)
                    ins = pe.transpose(misc_bf[0:PARTS * 16, 0:P], max_parts[:].rearrange("p i n -> p (i n)"),
                                       ident_bf[:])
                if what == "mean":
                    pe.wait_ge(s_y_mv, b + 1)
                    ins = pe.matmul(misc[:, 0:1], mean_mat[:], y_mv[:, 0:1], start=True, stop=True)
                if what == "var":
                    pe.wait_ge(s_y_sq, b + 1)
                    ins = pe.matmul(misc[:, 0:1], mean_mat[:], y_sq[:], start=True, stop=True)
                if what == "z_turn":
                    pe.wait_ge(s_z, b + 1)
                    for t in range(TT):
                        ins = pe.transpose(misc[:, P * t:P * t + P], z[:, P * t:P * t + P], ident[:])
                ins.then_inc(s_misc_full, 1)

            def pass_a(b, par, r, h):
                n, c = 4 * (r // 4) + h, r % 4
                m = b * STEPS + 4 * r + h
                if r + h == 0:
                    pe.wait_ge(s_q_relaid, b + 1)
                    pe.wait_ge(s_k_relaid, b + 1)
                if 4 * r + h >= 2 or later(b):
                    pe.wait_ge(s_max, m - 1)
                pe.matmul(score_a[h % 2][:], Qt[par][:, n, P * c:P * c + P], Kt[par][:, n],
                          start=True, stop=True).then_inc(s_a, 1)

            def pass_b(b, par, j, h):
                n, c = 4 * (j // 4) + h, j % 4
                m = b * STEPS + 4 * j + h
                if c == 0 and h == 0:
                    g = j // 4
                    pe.wait_ge(s_max_loaded[g % 2], (2 * b + g // 2 + 1) * DMA)
                if j or later(b):
                    pe.wait_ge(s_exp, m - 3)
                pe.matmul(score_b[h][:], Kt[par][:, n, P * c:P * c + P], Qt[par][:, n],
                          start=True, stop=True).then_inc(s_b, 1)

            def values(b, par, j):
                g, c = j // 4, j % 4
                pe.wait_ge(s_exp, b * STEPS + 4 * j + 4)
                if j == 0:
                    pe.wait_ge(s_v_relaid, b + 1)
                if c == 0 and (g or later(b)):
                    pe.wait_ge(s_o, 4 * b + g)
                for h in range(4):
                    ins = pe.matmul(pv_bank[32 * h:32 * h + 2 * DK, :], Vt[:, par, 4 * (4 * g + h) + c], probs[:, 4 * (j % 2) + h],
                                    start=(c == 0), stop=(c == 3), tile_position=(0, 32 * h))
                ins.then_inc(s_pv, 1)

            def stage(b, par):
                for r in range(QUADS):
                    for h in range(4):
                        if has(b, 0, NB - 1):
                            pass_a(b, par, r, h)
                        if r < LAG and has(b, 1, NB):
                            pass_b(b - 1, 1 - par, r + LAG, h)
                        if r >= LAG and has(b, 0, NB - 1):
                            pass_b(b, par, r - LAG, h)
                    if r <= LAG and has(b, 1, NB):
                        values(b - 1, 1 - par, r + LAG - 1)
                    if r > LAG and has(b, 0, NB - 1):
                        values(b, par, r - LAG - 1)
                    for q, what, db, g in misc_uses(5):
                        if q == r and has(b, max(0, 5 - db), NB - 1 + 5 - db):
                            fill(what, b + (db - 5), g)

            for what in ("x_turn", "q", "k", "v"):
                fill(what, 0)
            over_stages(pe, stage)

            def f_piece(b, par, e):
                if e == 2:
                    if later(b):
                        pe.wait_ge(s_f_read, 4 * b)
                    pe.wait_ge(s_f_norm, b + 1)
                    for t in range(TT):
                        ins = pe.transpose(misc[:, P * t:P * t + P], f_norm[:, t], ident[:])
                    ins.then_inc(s_f_full, 1)
                if e == 3:
                    pe.wait_ge(s_f_read, 4 * b + 1)
                    for t in range(TT):
                        ins = pe.matmul(misc[:, E * t:E * t + E], h2T[par][:, P * t:P * t + P], gw_sb[:],
                                        start=True, stop=True)
                    ins.then_inc(s_f_full, 1)
                if e == 5:
                    pe.wait_ge(s_f_read, 4 * b + 2)
                    pe.wait_ge(s_wd, b + 1)
                    pe.transpose(misc[:, 0:P], w_dense[par][:].rearrange("p t e -> p (t e)"), ident[:])\
                        .then_inc(s_f_full, 1)
                if e == 6:
                    pe.wait_ge(s_f_read, 4 * b + 3)
                    for t in range(TT):
                        ins = pe.matmul(misc[:, P * t:P * t + P], w_rows[par][:], b3_sb[:, t],
                                        start=True, stop=True)
                    ins.then_inc(s_f_full, 1)

            def expert(b, par, e):
                for c in range(HC):
                    u = (b * E + e) * HC + c
                    if e or later(b):
                        pe.wait_ge(s_hid, u - 1)
                    pe.matmul(up_bank[2 * c][:], w1_sb[:, e, P * c:P * c + P], h2T[par], start=True, stop=True)
                    pe.matmul(up_bank[2 * c + 1][:], w2_sb[:, e, P * c:P * c + P], h2T[par],
                              start=True, stop=True).then_inc(s_up, 1)

            def down(b, par, e):
                w = b * E + e
                pe.wait_ge(s_hid, HC * (w + 1))
                if e >= 2 or later(b):
                    pe.wait_ge(s_acc, w - 1)
                for t in range(TT):
                    for c in range(HC):
                        ins = pe.matmul(down_bank[e % 2][:, P * t:P * t + P],
                                        hidden[HC * (e % 2) + c][:, P * t:P * t + P], w3_sb[:, e, c],
                                        start=(c == 0), stop=(c == HC - 1))
                ins.then_inc(s_down, 1)

            def f_batch(b, par, ahead):
                for e in range(E):
                    expert(b, par, e)
                    if e:
                        down(b, par, e - 1)
                    if ahead:
                        f_piece(b + 1, 1 - par, e)
                down(b, par, E - 1)

            pe.wait_ge(s_expert_w, (4 + HC + TT) * DMA)
            pe.wait_ge(s_max, NB * STEPS)
            pe.wait_ge(s_exp, NB * STEPS)
            pe.wait_ge(s_misc_read, len(MISC))
            for e in range(E):
                f_piece(0, 0, e)
            f_batch(0, 0, True)
            f_batch(1, 1, True)
            with pe.Fori(1, NB // 2 - 1, 1) as i:
                f_batch(2 * i, 0, True)
                f_batch(2 * i + 1, 1, True)
            f_batch(NB - 2, 0, True)
            f_batch(NB - 1, 1, False)


def kernel(**inputs):
    import concourse.bacc as _bacc
    from concourse.bass_utils import run_bass_kernel_spmd as _run

    nc = _bacc.Bacc("TRN2", target_bir_lowering=False, num_devices=1)
    a = {n: np.asarray(v) for n, v in inputs.items()}
    wv = a["L0_attn_Wv"].reshape(4, 4, DK, D).transpose(1, 0, 2, 3).reshape(D, D)
    laid = {
        "x": a["L0_attn_x"], "wqT": a["L0_attn_Wq"].T, "wkT": a["L0_attn_Wk"].T, "wvT": wv.T,
        "w1": a["L0_ffn_w1"], "b1T": a["L0_ffn_b1"].T, "w2": a["L0_ffn_w2"], "b2T": a["L0_ffn_b2"].T,
        "w3": a["L0_ffn_w3"], "b3": a["L0_ffn_b3"], "gate_w": a["L0_ffn_gate_w"],
        "cT": a["L0_c"].T, "wmod": a["L0_wmod"],
    }
    laid = {f"in_{n}": np.ascontiguousarray(v) for n, v in laid.items()}
    args = {n[3:]: nc.dram_tensor(n, v.shape, F32, kind="ExternalInput").ap() for n, v in laid.items()}
    args["out"] = nc.dram_tensor("out", (NB, S, D), F32, kind="ExternalOutput").ap()
    build(nc, **args)
    return _run(nc, [laid], core_ids=[0]).results[0]["out"]
```

```python
from contextlib import ExitStack

import numpy as np
import concourse.bass as bass
from concourse import mybir

F32 = mybir.dt.float32
BF16 = mybir.dt.bfloat16
U32 = mybir.dt.uint32
I32 = mybir.dt.int32
ALU = mybir.AluOpType
ACT = mybir.ActivationFunctionType
AX_X = mybir.AxisListType.X

P = 128
NB, S, D = 16, 512, 128
HEADS, DK = 16, 8
G = D // DK
TOK = S // HEADS
PARTS = 3
ROWS = PARTS * PARTS * DK
MROW = 96
QUADS = 16
STEPS = 4 * QUADS
LAG = 9
TT = S // P
E, HID = 8, 256
HC = HID // P
EPS = 1e-5
DMA = 16


def misc_uses(b):
    uses = [
        (1, "max_rows", b - 1, 3), (2, "x_turn", b + 1, 0), (3, "q", b + 1, 0), (4, "mean", b - 2, 0),
        (5, "max_rows", b, 0), (6, "k", b + 1, 0), (7, "v", b + 1, 0), (8, "var", b - 2, 0),
        (9, "max_rows", b, 1), (11, "z_turn", b - 2, 0), (13, "max_rows", b, 2),
    ]
    return [u for u in uses if 0 <= u[2] < NB]


def misc_table():
    order = [("x_turn", 0, 0), ("q", 0, 0), ("k", 0, 0), ("v", 0, 0)]
    for b in range(NB + 2):
        order += [u[1:] for u in misc_uses(b)]
    return {u: n for n, u in enumerate(order)}


MISC = misc_table()
MISC_PER_STAGE = len(misc_uses(5))


def misc_index(what, b, g=0):
    if isinstance(b, int):
        return MISC[(what, b, g)]
    return (b - 5) * MISC_PER_STAGE + MISC[(what, 5, g)]


def build(nc, x, wqT, wkT, wvT, w1, b1T, w2, b2T, w3, b3, gate_w, cT, wmod, out):
    ctx = ExitStack()
    with ctx:
        def sb(name, shape, dt=F32):
            return ctx.enter_context(nc.sbuf_tensor(name, shape, dt))

        def sem(name):
            return ctx.enter_context(nc.semaphore(name))

        def dram(name, shape, dt=F32):
            return nc.dram_tensor(name, shape, dt, kind="Internal").ap()

        q_dram = dram("q_dram", [PARTS, DK, G, S], BF16)
        k_dram = dram("k_dram", [PARTS, DK, G, S], BF16)
        v_dram = dram("v_dram", [S, D])
        h_dram = dram("h_dram", [NB, D, S])
        o_dram = dram("o_dram", [2, 2 * DK, G, S])
        x2_dram = dram("x2_dram", [NB, S, D])
        gb_dram = dram("gb_dram", [NB, D])

        ident = sb("ident", [P, P])
        ident_bf = sb("ident_bf", [P, P], BF16)
        mean_mat = sb("mean_mat", [P, P])
        neg_half = sb("neg_half", [P, TT])
        iota8 = sb("iota8", [P, E])
        wq_sb = sb("wq_sb", [P, D])
        wk_sb = sb("wk_sb", [P, D])
        wv_sb = sb("wv_sb", [P, D])
        w1_sb = sb("w1_sb", [P, E, HID])
        w2_sb = sb("w2_sb", [P, E, HID])
        w3_sb = sb("w3_sb", [P, E, HC, D])
        b1_sb = sb("b1_sb", [P, HC, E])
        b2_sb = sb("b2_sb", [P, HC, E])
        b3_sb = sb("b3_sb", [P, TT, D])
        gw_sb = sb("gw_sb", [P, E])
        wmod_sb = sb("wmod_sb", [P, 6, D])
        c_sb = sb("c_sb", [P, NB])
        c_silu = sb("c_silu", [P, NB])
        mod = sb("mod", [P, 6, NB])
        mod_abs = sb("mod_abs", [P, 2, NB])
        mod_sign = sb("mod_sign", [P, 2, NB])
        gb_rows = sb("gb_rows", [NB, D])

        Qt = [sb(f"Qt{i}", [P, HEADS, S], BF16) for i in range(2)]
        Kt = [sb(f"Kt{i}", [P, HEADS, S], BF16) for i in range(2)]
        q_land = sb("q_land", [P, G, S], BF16)
        k_land = sb("k_land", [P, G, S], BF16)
        v_land = sb("v_land", [P, HEADS * 4, DK])
        Vt = sb("Vt", [P, 2, HEADS * 4, 2 * DK])
        probs = sb("probs", [P, 8, S])
        x_in = sb("x_in", [P, TT, D])
        x_stats = sb("x_stats", [P, TT, 6])
        x_mv = sb("x_mv", [P, TT, 2])
        x_ve = sb("x_ve", [P, TT])
        x_rstd = sb("x_rstd", [P, TT])
        x_shift = sb("x_shift", [P, TT])
        x_norm = sb("x_norm", [P, TT, D])
        hT = sb("hT", [P, S])
        q_f = sb("q_f", [P, S])
        k_f = sb("k_f", [P, S])
        v_f = sb("v_f", [P, TT, D])
        q_rest = sb("q_rest", [P, S])
        k_rest = sb("k_rest", [P, S])
        q_parts = sb("q_parts", [P, PARTS, S], BF16)
        k_parts = sb("k_parts", [P, PARTS, S], BF16)
        neg_max = sb("neg_max", [P, 2, 16])
        max_rest = sb("max_rest", [P, 16])
        max_parts = sb("max_parts", [P, PARTS, 16], BF16)
        max_rows = sb("max_rows", [PARTS * 16, P], BF16)
        o_sb = sb("o_sb", [P, 2, S])
        num_den = sb("num_den", [P, 2, S])
        h_back = sb("h_back", [P, S])
        x_back = sb("x_back", [P, TT, D])
        den_inv = sb("den_inv", [P, S])
        attn = sb("attn", [P, S])
        y = sb("y", [P, S])
        y_stats = sb("y_stats", [P, 6])
        y_mv = sb("y_mv", [P, 2])
        y_mean = sb("y_mean", [P, 1])
        y_dev = sb("y_dev", [P, 1])
        y_dev2 = sb("y_dev2", [P, 1])
        y_sq = sb("y_sq", [P, 1])
        y_ve = sb("y_ve", [P, 1])
        y_rstd = sb("y_rstd", [P, 1])
        y_scale = sb("y_scale", [P, 1])
        y_shift = sb("y_shift", [P, 1])
        z = sb("z", [P, S])
        x2_out = sb("x2_out", [P, TT, D])
        room_q = Qt[0][:].rearrange("p n q -> p (n q)").bitcast(F32)
        room_k = Kt[0][:].rearrange("p n q -> p (n q)").bitcast(F32)
        hidden = [room_q[:, i * S:(i + 1) * S] for i in range(4)]
        gate_act = room_q[:, 4 * S:6 * S].rearrange("p (c s) -> p c s", c=HC)
        acc = room_q[:, 6 * S:8 * S].rearrange("p (i t c) -> p i t c", i=2, t=TT)
        x2 = room_k[:, 0:2 * S].rearrange("p (i t c) -> p i t c", i=2, t=TT)
        y_out = room_k[:, 2 * S:4 * S].rearrange("p (i t c) -> p i t c", i=2, t=TT)
        h2T = [room_k[:, (4 + i) * S:(5 + i) * S] for i in range(2)]
        f_norm = room_k[:, 6 * S:7 * S].rearrange("p (t c) -> p t c", t=TT)
        gb_all = sb("gb_all", [P, 2, D])
        f_stats = sb("f_stats", [P, TT, 6])
        f_mv = sb("f_mv", [P, TT, 2])
        f_ve = sb("f_ve", [P, TT])
        f_rstd = sb("f_rstd", [P, TT])
        f_shift = sb("f_shift", [P, TT])
        logits = sb("logits", [P, TT, E])
        top = sb("top", [P, TT, 8])
        top_at = sb("top_at", [P, TT, 8], U32)
        top_at_f = sb("top_at_f", [P, TT, 2])
        top_gap = sb("top_gap", [P, TT])
        top_tanh = sb("top_tanh", [P, TT])
        score = sb("score", [P, 2, TT])
        pick = sb("pick", [P, 2, TT, E])
        w_dense = [sb(f"w_dense{i}", [P, TT, 32]) for i in range(2)]
        w_rows = [sb(f"w_rows{i}", [P, P]) for i in range(2)]

        bank = [ctx.enter_context(nc.psum_tensor(f"bank{i}", [P, S], F32)) for i in range(8)]
        score_a = bank[0:3]
        score_b = bank[3:6]
        pv_bank = bank[6]
        misc = bank[7]
        misc_bf = misc[:].bitcast(BF16)
        up_bank = bank[0:4]
        down_bank = bank[4:6]

        s_w = sem("s_w")
        s_expert_w = sem("s_expert_w")
        s_const = sem("s_const")
        s_clear = sem("s_clear")
        s_c_silu = sem("s_c_silu")
        s_mod_mm = sem("s_mod_mm")
        s_mod_chain = sem("s_mod_chain")
        s_mod = sem("s_mod")
        s_gb_mm = sem("s_gb_mm")
        s_gb = sem("s_gb")
        s_gb_dram = sem("s_gb_dram")
        s_misc_full = sem("s_misc_full")
        s_misc_read = sem("s_misc_read")
        s_x_in = sem("s_x_in")
        s_x_stats = sem("s_x_stats")
        s_x_mv = sem("s_x_mv")
        s_x_ve = sem("s_x_ve")
        s_x_rstd = sem("s_x_rstd")
        s_x_shift = sem("s_x_shift")
        s_x_norm = sem("s_x_norm")
        s_h_stored = sem("s_h_stored")
        s_split_q = [sem(f"s_split_q{i}") for i in range(4)]
        s_split_k = [sem(f"s_split_k{i}") for i in range(4)]
        s_q_stored = sem("s_q_stored")
        s_k_stored = sem("s_k_stored")
        s_v_stored = sem("s_v_stored")
        s_q_landed = sem("s_q_landed")
        s_k_landed = sem("s_k_landed")
        s_q_relaid = sem("s_q_relaid")
        s_k_relaid = sem("s_k_relaid")
        s_v_relaid = sem("s_v_relaid")
        s_v_loaded = sem("s_v_loaded")
        s_a = sem("s_a")
        s_max = sem("s_max")
        s_split_max = [sem(f"s_split_max{i}") for i in range(4)]
        s_max_moved = sem("s_max_moved")
        s_b = sem("s_b")
        s_exp = sem("s_exp")
        s_pv = sem("s_pv")
        s_o = sem("s_o")
        s_o_stored = [sem(f"s_o_stored{i}") for i in range(2)]
        s_back = sem("s_back")
        s_x_back = sem("s_x_back")
        s_den_inv = sem("s_den_inv")
        s_attn = sem("s_attn")
        s_y = sem("s_y")
        s_y_stats = sem("s_y_stats")
        s_y_mv = sem("s_y_mv")
        s_y_dev = sem("s_y_dev")
        s_y_dev2 = sem("s_y_dev2")
        s_y_sq = sem("s_y_sq")
        s_y_rstd = sem("s_y_rstd")
        s_y_scale = sem("s_y_scale")
        s_y_shift = sem("s_y_shift")
        s_z = sem("s_z")
        s_x2_stored = sem("s_x2_stored")
        s_x2 = [sem(f"s_x2_{i}") for i in range(2)]
        s_f_stats = sem("s_f_stats")
        s_f_mv = sem("s_f_mv")
        s_f_ve = sem("s_f_ve")
        s_f_rstd = sem("s_f_rstd")
        s_f_shift = sem("s_f_shift")
        s_f_norm = sem("s_f_norm")
        s_f_full = sem("s_f_full")
        s_f_read = sem("s_f_read")
        s_top = sem("s_top")
        s_top_at = sem("s_top_at")
        s_gap = sem("s_gap")
        s_tanh = sem("s_tanh")
        s_score = sem("s_score")
        s_pick = sem("s_pick")
        s_wd = sem("s_wd")
        s_up = sem("s_up")
        s_act = sem("s_act")
        s_hid = sem("s_hid")
        s_down = sem("s_down")
        s_acc = sem("s_acc")
        s_scaled = sem("s_scaled")
        s_fin = sem("s_fin")
        s_out = [sem(f"s_out{i}") for i in range(2)]

        block = ctx.enter_context(nc.Block())

        def over_stages(eng, stage):
            stage(0, 0)
            stage(1, 1)
            with eng.Fori(1, NB // 2 - 1, 1) as i:
                stage(2 * i, 0)
                stage(2 * i + 1, 1)
            for b in range(NB - 2, NB + 2):
                stage(b, b % 2)

        def has(b, first, last):
            return not isinstance(b, int) or first <= b <= last

        def later(b, n=1):
            return not isinstance(b, int) or b >= n

        N_CONST = 11

        def wait_apart(eng, semaphore, value):
            if isinstance(value, bass.RuntimeValue):
                value = eng.to_reg(value)
            eng.wait_ge(s_const, N_CONST)
            eng.wait_ge(semaphore, value)

        @block.sync
        def _(sp):
            for dst, src in (
                (wmod_sb[:].rearrange("p j c -> p (j c)"), wmod), (c_sb[:], cT),
                (wq_sb[:], wqT), (wk_sb[:], wkT), (wv_sb[:], wvT), (gw_sb[:], gate_w),
            ):
                sp.dma_start(dst, src).then_inc(s_w, DMA)

            def x_load(b):
                if later(b):
                    wait_apart(sp, s_x_norm, b)
                sp.dma_start(x_in[:], x[b].rearrange("(t p) c -> p t c", p=P)).then_inc(s_x_in, DMA)

            def front_store(b, what):
                if what == "x_turn":
                    wait_apart(sp, s_misc_read, misc_index("x_turn", b) + 1)
                    sp.dma_start(h_dram[b], hT[:]).then_inc(s_h_stored, DMA)
                if what == "q":
                    sp.wait_ge(s_split_q[3], b + 1)
                    for i in range(PARTS):
                        sp.dma_start(q_dram[i].rearrange("d g s -> g d s"), q_parts[:, i]).then_inc(s_q_stored, DMA)
                if what == "k":
                    sp.wait_ge(s_split_k[3], b + 1)
                    for i in range(PARTS):
                        sp.dma_start(k_dram[i].rearrange("d g s -> g d s"), k_parts[:, i]).then_inc(s_k_stored, DMA)
                if what == "v":
                    sp.wait_ge(s_misc_read, misc_index("v", b) + 1)
                    sp.dma_start(v_dram.rearrange("(t p) c -> p t c", p=P), v_f[:]).then_inc(s_v_stored, DMA)

            def q_load(b):
                if later(b):
                    wait_apart(sp, s_q_relaid, 8 * b)
                sp.wait_ge(s_q_stored, (b + 1) * PARTS * DMA)
                for i in range(PARTS):
                    row = i * PARTS * DK
                    sp.dma_start(q_land[row:row + PARTS * DK],
                                 q_dram[i:i + 1].rearrange("i d g s -> i d (g s)").broadcast_to([PARTS, DK, G * S]))\
                        .then_inc(s_q_landed, DMA)

            def k_load(b):
                if later(b):
                    wait_apart(sp, s_k_relaid, 4 * b)
                sp.wait_ge(s_k_stored, (b + 1) * PARTS * DMA)
                for i in range(PARTS):
                    row = i * PARTS * DK
                    sp.dma_start(k_land[row:row + PARTS * DK], k_dram.rearrange("j d g s -> (j d) g s"))\
                        .then_inc(s_k_landed, DMA)

            def v_load(b):
                if later(b):
                    wait_apart(sp, s_v_relaid, b)
                sp.wait_ge(s_v_stored, (b + 1) * DMA)
                for g in range(4):
                    sp.dma_start(
                        v_land[32 * g:32 * g + TOK].rearrange("p (n i) d -> p n (i d)", n=HEADS),
                        v_dram.rearrange("(n p) (g w) -> g p n w", p=TOK, g=4)[g]).then_inc(s_v_loaded, DMA)

            def max_move(b, par, g):
                sp.wait_ge(s_misc_read, misc_index("max_rows", b, g) + 1)
                for i in range(PARTS):
                    sp.dma_start(Qt[par][MROW + i:MROW + i + 1, 4 * g:4 * g + 4]
                                 .rearrange("o h (c p) -> o (h c) p", p=P), max_rows[16 * i:16 * i + 16])\
                        .then_inc(s_max_moved, DMA)

            def o_store(b, par, g):
                sp.wait_ge(s_o, 4 * b + g + 1)
                for h in range(4):
                    sp.dma_start(
                        o_dram[par, :, :, P * g + TOK * h:P * g + TOK * h + TOK],
                        o_sb[32 * h:32 * h + 2 * DK, g % 2, :].rearrange("d (g s) -> d g s", s=TOK))\
                        .then_inc(s_o_stored[g % 2], DMA)

            def back_load(b, par):
                for i in range(2):
                    sp.wait_ge(s_o_stored[i], (b + 1) * 8 * DMA)
                if later(b):
                    sp.wait_ge(s_y, b)
                for w in range(2):
                    sp.dma_start(num_den[:, w], o_dram[par, w * DK:w * DK + DK].rearrange("d g s -> g d s"))\
                        .then_inc(s_back, DMA)
                wait_apart(sp, s_h_stored, (b + 1) * DMA)
                sp.dma_start(h_back[:], h_dram[b]).then_inc(s_back, DMA)

            def x_back_load(b):
                if later(b):
                    wait_apart(sp, s_misc_read, misc_index("z_turn", b - 1) + 1)
                sp.dma_start(x_back[:], x[b].rearrange("(t p) c -> p t c", p=P)).then_inc(s_x_back, DMA)

            def x2_store(b):
                wait_apart(sp, s_misc_read, misc_index("z_turn", b) + 1)
                sp.dma_start(x2_dram[b].rearrange("(t p) c -> p t c", p=P), x2_out[:]).then_inc(s_x2_stored, DMA)

            def stage(b, par):
                if has(b, 1, NB):
                    max_move(b - 1, 1 - par, 3)
                    o_store(b - 1, 1 - par, 1)
                if has(b, 0, NB - 2):
                    front_store(b + 1, "x_turn")
                if has(b, 0, NB - 3):
                    x_load(b + 2)
                if has(b, 0, NB - 1):
                    max_move(b, par, 0)
                if has(b, 2, NB + 1):
                    x_back_load(b - 2)
                if has(b, 1, NB):
                    o_store(b - 1, 1 - par, 2)
                if has(b, 0, NB - 2):
                    front_store(b + 1, "q")
                    q_load(b + 1)
                    front_store(b + 1, "v")
                    front_store(b + 1, "k")
                if has(b, 0, NB - 1):
                    max_move(b, par, 1)
                if has(b, 0, NB - 2):
                    k_load(b + 1)
                if has(b, 1, NB):
                    o_store(b - 1, 1 - par, 3)
                if has(b, 0, NB - 2):
                    v_load(b + 1)
                if has(b, 1, NB):
                    back_load(b - 1, 1 - par)
                if has(b, 2, NB + 1):
                    x2_store(b - 2)
                if has(b, 0, NB - 1):
                    max_move(b, par, 2)
                    o_store(b, par, 0)

            x_load(0)
            for dst, src in (
                (w1_sb[:], w1.rearrange("e i h -> i e h")), (w2_sb[:], w2.rearrange("e i h -> i e h")),
                (b1_sb[:], b1T.rearrange("(c p) e -> p c e", p=P)),
                (b2_sb[:], b2T.rearrange("(c p) e -> p c e", p=P)),
            ):
                sp.dma_start(dst, src).then_inc(s_expert_w, DMA)
            for c in range(HC):
                sp.dma_start(w3_sb[:, :, c], w3[:, c * P:(c + 1) * P].rearrange("e p d -> p e d")).then_inc(s_expert_w, DMA)
            sp.wait_ge(s_const, N_CONST)
            for t in range(TT):
                sp.dma_start(b3_sb[32 * t:32 * t + E, t], b3).then_inc(s_expert_w, DMA)
            front_store(0, "x_turn")
            x_load(1)
            sp.wait_ge(s_clear, 4)
            front_store(0, "q")
            q_load(0)
            front_store(0, "v")
            front_store(0, "k")
            k_load(0)
            v_load(0)
            over_stages(sp, stage)

            def f_load(b, par):
                if later(b, 2):
                    wait_apart(sp, s_fin, b - 1)
                sp.dma_start(x2[:, par], x2_dram[b].rearrange("(t p) c -> p t c", p=P)).then_inc(s_x2[par], DMA)
                sp.dma_start(gb_all[:, par], gb_dram[bass.ds(b, 1)].broadcast_to([P, D])).then_inc(s_x2[par], DMA)

            def f_store(b, par):
                wait_apart(sp, s_fin, b + 1)
                sp.dma_start(out[b].rearrange("(t p) c -> p t c", p=P), y_out[:, par]).then_inc(s_out[par], DMA)

            sp.wait_ge(s_gb, 1)
            sp.dma_start(gb_dram, gb_rows[:]).then_inc(s_gb_dram, DMA)
            sp.wait_ge(s_gb_dram, DMA)
            sp.wait_ge(s_x2_stored, NB * DMA)
            f_load(0, 0)
            f_load(1, 1)
            with sp.Fori(0, NB // 2 - 1, 1) as i:
                for par in range(2):
                    f_store(2 * i + par, par)
                    f_load(2 * i + par + 2, par)
            for b in (NB - 2, NB - 1):
                f_store(b, b % 2)
            for par in range(2):
                sp.wait_ge(s_out[par], NB // 2 * DMA)

        @block.gpsimd
        def _(pool):
            pool.memset(ident[:], 0.0).then_inc(s_const, 1)
            pool.memset(ident_bf[:], 0.0).then_inc(s_const, 1)
            pool.memset(mean_mat[:], 1.0 / P).then_inc(s_const, 1)
            pool.memset(neg_half[:], -0.5).then_inc(s_const, 1)
            pool.iota(iota8[:], [[1, E]], base=0, channel_multiplier=0,
                      allow_small_or_imprecise_dtypes=True).then_inc(s_const, 1)
            pool.memset(Vt[:], 1.0).then_inc(s_const, 1)
            pool.memset(b3_sb[:], 0.0).then_inc(s_const, 1)
            pool.wait_ge(s_const, 7)
            for m in (ident, ident_bf):
                pool.affine_select(out=m[:], in_=m[:], compare_op=ALU.not_equal, fill=1.0, base=0,
                                   pattern=[[-1, P]], channel_multiplier=1).then_inc(s_const, 1)
            for i in range(2):
                pool.memset(w_dense[i][:], 0.0).then_inc(s_const, 1)

            def split(src, rest, parts, done, k):
                pool.tensor_copy(parts[:, 0], src).then_inc(done[0], 1)
                pool.wait_ge(done[0], k + 1)
                pool.tensor_tensor(rest, src, parts[:, 0], ALU.subtract).then_inc(done[1], 1)
                wait_apart(pool, done[1], k + 1)
                pool.tensor_copy(parts[:, 1], rest).then_inc(done[2], 1)
                pool.wait_ge(done[2], k + 1)
                pool.tensor_tensor(parts[:, 2], rest, parts[:, 1], ALU.subtract).then_inc(done[3], 1)

            def split_q(b):
                wait_apart(pool, s_misc_read, misc_index("q", b) + 1)
                if later(b):
                    wait_apart(pool, s_q_stored, b * PARTS * DMA)
                split(q_f[:], q_rest[:], q_parts, s_split_q, b)

            def split_k(b):
                wait_apart(pool, s_misc_read, misc_index("k", b) + 1)
                if later(b):
                    wait_apart(pool, s_k_stored, b * PARTS * DMA)
                split(k_f[:], k_rest[:], k_parts, s_split_k, b)

            def split_max(b, g):
                gg = 4 * b + g
                pool.wait_ge(s_max, (gg + 1) * 16)
                if g or later(b):
                    pb, pg = (b, g - 1) if g else (b - 1, 3)
                    wait_apart(pool, s_misc_full, misc_index("max_rows", pb, pg) + 1)
                split(neg_max[:, g % 2], max_rest[:], max_parts, s_split_max, gg)

            def relay_k(b, par, g):
                wait_apart(pool, s_k_landed, (b + 1) * PARTS * DMA)
                if g == 0 and later(b, 2):
                    wait_apart(pool, s_b, (b - 1) * STEPS)
                pool.tensor_copy(
                    Kt[par][:].rearrange("p n q -> p (n q)").bitcast(I32)
                    .rearrange("p (n g s) -> p n g s", n=HEADS, g=G)[:, 4 * g:4 * g + 4],
                    k_land[:].rearrange("p g s -> p (g s)").bitcast(I32)
                    .rearrange("p (g n s) -> p n g s", n=HEADS, g=G)[:, 4 * g:4 * g + 4]).then_inc(s_k_relaid, 1)

            def relay_v(b, par):
                wait_apart(pool, s_v_loaded, (b + 1) * 4 * DMA)
                if later(b, 2):
                    wait_apart(pool, s_pv, (b - 1) * QUADS)
                pool.tensor_copy(Vt[:, par, :, 0:DK], v_land[:]).then_inc(s_v_relaid, 1)

            def x_power(b):
                pool.wait_ge(s_x_ve, b + 1)
                pool.tensor_tensor(x_rstd[:], x_ve[:], neg_half[:], ALU.pow).then_inc(s_x_rstd, 1)

            def y_power(b):
                pool.wait_ge(s_misc_read, misc_index("var", b) + 1)
                pool.tensor_tensor(y_rstd[:], y_ve[:], neg_half[:, 0:1], ALU.pow).then_inc(s_y_rstd, 1)

            def add_h(b):
                pool.wait_ge(s_den_inv, b + 1)
                pool.tensor_tensor(attn[:], num_den[:, 0], den_inv[:], ALU.mult).then_inc(s_attn, 1)
                pool.wait_ge(s_attn, b + 1)
                if later(b):
                    pool.wait_ge(s_z, b)
                pool.tensor_tensor(y[:], attn[:], h_back[:], ALU.add).then_inc(s_y, 1)

            def stage(b, par):
                if has(b, 1, NB):
                    split_max(b - 1, 3)
                if has(b, 0, NB - 2):
                    x_power(b + 1)
                if has(b, 2, NB + 1):
                    add_h(b - 2)
                if has(b, 0, NB - 1):
                    relay_k(b, par, 2)
                    relay_k(b, par, 3)
                    split_max(b, 0)
                if has(b, 0, NB - 2):
                    split_q(b + 1)
                if has(b, 0, NB - 1):
                    relay_v(b, par)
                if has(b, 0, NB - 2):
                    split_k(b + 1)
                if has(b, 0, NB - 1):
                    split_max(b, 1)
                if has(b, 2, NB + 1):
                    y_power(b - 2)
                if has(b, 0, NB - 2):
                    relay_k(b + 1, 1 - par, 0)
                if has(b, 0, NB - 1):
                    split_max(b, 2)
                if has(b, 0, NB - 2):
                    relay_k(b + 1, 1 - par, 1)

            x_power(0)
            split_q(0)
            split_k(0)
            relay_k(0, 0, 0)
            relay_k(0, 0, 1)
            over_stages(pool, stage)

            with pool.Fori(0, NB, 1) as b:
                pool.wait_ge(s_f_ve, b + 1)
                pool.tensor_tensor(f_rstd[:], f_ve[:], neg_half[:], ALU.pow).then_inc(s_f_rstd, 1)

        @block.vector
        def _(dve):
            for t in (q_land, k_land):
                dve.memset(t[:].rearrange("p g s -> p (g s)").bitcast(I32), 0).then_inc(s_clear, 1)
            dve.memset(pv_bank[:], 0.0).then_inc(s_clear, 1)
            dve.wait_ge(s_clear, 2)
            dve.memset(k_land[MROW:MROW + PARTS], 1.0).then_inc(s_clear, 1)

            link_count = [0]

            def link(ins):
                link_count[0] += 1
                ins.then_inc(s_mod_chain, 1)
                dve.wait_ge(s_mod_chain, link_count[0])

            dve.wait_ge(s_mod_mm, 1)
            link(dve.tensor_copy(mod[:].rearrange("p j b -> p (j b)"), misc[:, 0:6 * NB]))
            gates = mod[:].rearrange("p (k j) b -> p k j b", j=3)[:, :, 2]
            scales = mod[:].rearrange("p (k j) b -> p k j b", j=3)[:, :, 1]
            link(dve.tensor_scalar(scales, scales, 1.0, None, ALU.add))
            link(dve.tensor_scalar(mod_sign[:], gates, 0.0, 2.0, ALU.is_ge, ALU.mult))
            link(dve.tensor_scalar(mod_sign[:], mod_sign[:], 1.0, None, ALU.subtract))
            link(dve.tensor_tensor(mod_abs[:], mod_sign[:], gates, ALU.mult))
            link(dve.tensor_scalar(mod_abs[:], mod_abs[:], 0.25, None, ALU.max))
            dve.tensor_tensor(gates, mod_sign[:], mod_abs[:], ALU.mult).then_inc(s_mod, 1)
            dve.wait_ge(s_gb_mm, 1)
            dve.tensor_copy(gb_rows[:], misc[0:NB, 0:D]).then_inc(s_gb, 1)

            def stats(src, st, mv, ve, k, s_st, s_mv, s_ve):
                for t in range(TT):
                    dve.bn_stats(st[:, t], src[:, t]).then_inc(s_st, 1)
                wait_apart(dve, s_st, TT * (k + 1))
                for t in range(TT):
                    dve.bn_aggr(mv[:, t], st[:, t]).then_inc(s_mv, 1)
                dve.wait_ge(s_mv, TT * (k + 1))
                dve.tensor_scalar(ve[:], mv[:, :, 1], EPS, None, ALU.add).then_inc(s_ve, 1)

            def normalise(src, dst, mv, rs, shift, k, s_shift, done):
                dve.scalar_tensor_tensor(shift[:], mv[:, :, 0], -1.0, rs[:], ALU.mult, ALU.mult)\
                    .then_inc(s_shift, 1)
                dve.wait_ge(s_shift, k + 1)
                for t in range(TT):
                    ins = dve.tensor_scalar(dst[:, t], src[:, t], rs[:, t:t + 1], shift[:, t:t + 1],
                                            ALU.mult, ALU.add)
                ins.then_inc(done, 1)

            def front_stats(b):
                dve.wait_ge(s_x_in, (b + 1) * DMA)
                stats(x_in, x_stats, x_mv, x_ve, b, s_x_stats, s_x_mv, s_x_ve)

            def front_norm(b):
                dve.wait_ge(s_x_rstd, b + 1)
                if later(b):
                    dve.wait_ge(s_misc_full, misc_index("x_turn", b - 1) + 1)
                normalise(x_in, x_norm, x_mv, x_rstd, x_shift, b, s_x_shift, s_x_norm)

            def maxima(b, r):
                g, c = r // 4, r % 4
                if c == 0 and (g >= 2 or later(b)):
                    dve.wait_ge(s_split_max[3], 4 * b + g - 1)
                for h in range(4):
                    dve.wait_ge(s_a, b * STEPS + 4 * r + h + 1)
                    dve.tensor_reduce(neg_max[:, g % 2, 4 * h + c:4 * h + c + 1], score_a[(4 * r + h) % 3][:],
                                      AX_X, ALU.max, negate=True).then_inc(s_max, 1)

            def end_inv(b):
                dve.wait_ge(s_back, (b + 1) * 3 * DMA)
                dve.reciprocal(den_inv[:], num_den[:, 1]).then_inc(s_den_inv, 1)

            def end_stats(b):
                dve.wait_ge(s_y, b + 1)
                dve.bn_stats(y_stats[:], y[:]).then_inc(s_y_stats, 1)
                wait_apart(dve, s_y_stats, b + 1)
                dve.bn_aggr(y_mv[:], y_stats[:]).then_inc(s_y_mv, 1)

            def end_dev(b):
                dve.wait_ge(s_misc_full, misc_index("mean", b) + 1)
                dve.tensor_copy(y_mean[:], misc[:, 0:1]).then_inc(s_misc_read, 1)
                dve.wait_ge(s_misc_read, misc_index("mean", b) + 1)
                dve.tensor_tensor(y_dev[:], y_mv[:, 0:1], y_mean[:], ALU.subtract).then_inc(s_y_dev, 1)
                dve.wait_ge(s_y_dev, b + 1)
                dve.tensor_tensor(y_dev2[:], y_dev[:], y_dev[:], ALU.mult).then_inc(s_y_dev2, 1)
                dve.wait_ge(s_y_dev2, b + 1)
                dve.tensor_tensor(y_sq[:], y_dev2[:], y_mv[:, 1:2], ALU.add).then_inc(s_y_sq, 1)

            def end_var(b):
                dve.wait_ge(s_misc_full, misc_index("var", b) + 1)
                dve.tensor_scalar(y_ve[:], misc[:, 0:1], EPS, None, ALU.add).then_inc(s_misc_read, 1)

            def end_z(b):
                dve.wait_ge(s_y_rstd, b + 1)
                dve.tensor_tensor(y_scale[:], mod[:, 2, bass.ds(b, 1)], y_rstd[:], ALU.mult).then_inc(s_y_scale, 1)
                dve.wait_ge(s_y_scale, b + 1)
                dve.scalar_tensor_tensor(y_shift[:], y_mean[:], -1.0, y_scale[:], ALU.mult, ALU.mult)\
                    .then_inc(s_y_shift, 1)
                dve.wait_ge(s_y_shift, b + 1)
                if later(b):
                    dve.wait_ge(s_misc_full, misc_index("z_turn", b - 1) + 1)
                dve.tensor_scalar(z[:], y[:], y_scale[:], y_shift[:], ALU.mult, ALU.add).then_inc(s_z, 1)

            def end_x2(b):
                dve.wait_ge(s_misc_full, misc_index("z_turn", b) + 1)
                if later(b):
                    dve.wait_ge(s_x2_stored, b * DMA)
                dve.wait_ge(s_x_back, (b + 1) * DMA)
                dve.tensor_tensor(x2_out[:].rearrange("p t c -> p (t c)"), misc[:],
                                  x_back[:].rearrange("p t c -> p (t c)"), ALU.add).then_inc(s_misc_read, 1)

            def stage(b, par):
                for r in range(QUADS):
                    if has(b, 0, NB - 2):
                        if r == 0:
                            front_stats(b + 1)
                        if r == 1:
                            front_norm(b + 1)
                    if has(b, 2, NB + 1):
                        if r == 3:
                            end_stats(b - 2)
                        if r == 5:
                            end_dev(b - 2)
                        if r == 9:
                            end_var(b - 2)
                        if r == 11:
                            end_z(b - 2)
                        if r == 12:
                            end_x2(b - 2)
                    if has(b, 0, NB - 1):
                        maxima(b, r)
                    if r == 15 and has(b, 1, NB):
                        end_inv(b - 1)

            front_stats(0)
            front_norm(0)
            over_stages(dve, stage)

            def f_piece(b, par, e):
                if e == 0:
                    dve.wait_ge(s_x2[par], (b - par + 2) * DMA)
                    stats(x2[:, par], f_stats, f_mv, f_ve, b, s_f_stats, s_f_mv, s_f_ve)
                if e == 1:
                    dve.wait_ge(s_f_rstd, b + 1)
                    if later(b):
                        dve.wait_ge(s_f_full, 4 * b - 3)
                    normalise(x2[:, par], f_norm, f_mv, f_rstd, f_shift, b, s_f_shift, s_f_norm)
                if e == 3:
                    dve.wait_ge(s_f_full, 4 * b + 2)
                    dve.tensor_copy(logits[:].rearrange("p t e -> p (t e)"), misc[:, 0:TT * E])\
                        .then_inc(s_f_read, 1)
                    wait_apart(dve, s_f_read, 4 * b + 2)
                    for t in range(TT):
                        dve.max(top[:, t], logits[:, t]).then_inc(s_top, 1)
                    dve.wait_ge(s_top, TT * (b + 1))
                    if later(b):
                        dve.wait_ge(s_tanh, b)
                    dve.tensor_tensor(top_gap[:], top[:, :, 0], top[:, :, 1], ALU.subtract).then_inc(s_gap, 1)
                    for t in range(TT):
                        dve.max_index(top_at[:, t], top[:, t], logits[:, t]).then_inc(s_top_at, 1)
                if e == 4:
                    dve.wait_ge(s_top_at, (TT + 1) * b + TT)
                    dve.tensor_copy(top_at_f[:], top_at[:, :, 0:2]).then_inc(s_top_at, 1)
                    dve.wait_ge(s_tanh, b + 1)
                    for k in range(2):
                        dve.tensor_scalar(score[:, k], top_tanh[:], 0.5 - k, 0.5, ALU.mult, ALU.add)\
                            .then_inc(s_score, 1)
                    dve.wait_ge(s_top_at, (TT + 1) * (b + 1))
                    dve.wait_ge(s_score, 2 * (b + 1))
                    for k in range(2):
                        for t in range(TT):
                            dve.tensor_scalar(pick[:, k, t], iota8[:], top_at_f[:, t, k:k + 1],
                                              score[:, k, t:t + 1], ALU.is_equal, ALU.mult).then_inc(s_pick, 1)
                    dve.wait_ge(s_pick, 2 * TT * (b + 1))
                    dve.tensor_tensor(w_dense[par][:, :, 0:E], pick[:, 0], pick[:, 1], ALU.add).then_inc(s_wd, 1)
                if e == 6:
                    dve.wait_ge(s_f_full, 4 * b + 4)
                    dve.tensor_copy(acc[:, par].rearrange("p t c -> p (t c)"), misc[:]).then_inc(s_f_read, 1)

            def expert(b, par, e):
                for c in range(HC):
                    u = (b * E + e) * HC + c
                    slot = HC * (e % 2) + c
                    dve.wait_ge(s_act, u + 1)
                    if e >= 2 or later(b):
                        dve.wait_ge(s_down, b * E + e - 1)
                    dve.scalar_tensor_tensor(hidden[slot], up_bank[2 * c + 1][:], b2_sb[:, c, e:e + 1],
                                             gate_act[:, c], ALU.add, ALU.mult).then_inc(s_hid, 1)

            def add_expert(b, par, e):
                w = b * E + e
                dve.wait_ge(s_down, w + 1)
                if e or later(b):
                    dve.wait_ge(s_acc, w)
                if e == 0:
                    dve.wait_ge(s_f_read, 4 * b + 4)
                for t in range(TT):
                    ins = dve.scalar_tensor_tensor(acc[:, par, t], down_bank[e % 2][:, P * t:P * t + P],
                                                   w_dense[par][:, t, e:e + 1], acc[:, par, t],
                                                   ALU.mult, ALU.add)
                ins.then_inc(s_acc, 1)

            def finish(b, par):
                dve.wait_ge(s_acc, (b + 1) * E)
                if later(b, 2):
                    dve.wait_ge(s_out[par], (b - par) * (DMA // 2))
                dve.tensor_tensor(y_out[:, par], acc[:, par],
                                  gb_all[:, par].unsqueeze(1).broadcast_to([P, TT, D]), ALU.mult)\
                    .then_inc(s_scaled, 1)
                dve.wait_ge(s_scaled, b + 1)
                dve.tensor_tensor(y_out[:, par], y_out[:, par], x2[:, par], ALU.add).then_inc(s_fin, 1)

            def f_batch(b, par, ahead):
                for e in range(E):
                    expert(b, par, e)
                    if e:
                        add_expert(b, par, e - 1)
                    if ahead:
                        f_piece(b + 1, 1 - par, e)
                add_expert(b, par, E - 1)
                finish(b, par)

            for e in range(E):
                f_piece(0, 0, e)
            f_batch(0, 0, True)
            f_batch(1, 1, True)
            with dve.Fori(1, NB // 2 - 1, 1) as i:
                f_batch(2 * i, 0, True)
                f_batch(2 * i + 1, 1, True)
            f_batch(NB - 2, 0, True)
            f_batch(NB - 1, 1, False)

        @block.scalar
        def _(act):
            act.wait_ge(s_w, 6 * DMA)
            act.activation(c_silu[:], c_sb[:], ACT.Silu).then_inc(s_c_silu, 1)
            act.wait_ge(s_mod, 1)

            def evacuate(what, b, g=0):
                act.wait_ge(s_misc_full, misc_index(what, b, g) + 1)
                if what == "x_turn":
                    if later(b):
                        act.wait_ge(s_h_stored, b * DMA)
                    ins = act.activation(hT[:], misc[:], ACT.Identity, bias=mod[:, 0, bass.ds(b, 1)],
                                         scale=mod[:, 1, bass.ds(b, 1)])
                if what == "q":
                    if later(b):
                        act.wait_ge(s_split_q[1], b)
                    ins = act.activation(q_f[:], misc[:], ACT.Copy)
                if what == "k":
                    if later(b):
                        act.wait_ge(s_split_k[1], b)
                    ins = act.activation(k_f[:], misc[:], ACT.Copy)
                if what == "v":
                    if later(b):
                        act.wait_ge(s_v_stored, b * DMA)
                    ins = act.activation(v_f[:].rearrange("p t c -> p (t c)"), misc[:], ACT.Copy)
                if what == "max_rows":
                    if g or later(b):
                        act.wait_ge(s_max_moved, (4 * b + g) * PARTS * DMA)
                    ins = act.activation(max_rows[:], misc_bf[0:PARTS * 16, 0:P], ACT.Copy)
                ins.then_inc(s_misc_read, 1)

            def exps(b, j):
                if j >= 2 or later(b):
                    act.wait_ge(s_pv, b * QUADS + j - 1)
                for h in range(4):
                    n = b * STEPS + 4 * j + h
                    act.wait_ge(s_b, n + 1)
                    act.activation(probs[:, 4 * (j % 2) + h], score_b[(4 * j + h) % 3][:], ACT.Exp).then_inc(s_exp, 1)

            def relay_q(b, par, k):
                act.wait_ge(s_q_landed, (b + 1) * PARTS * DMA)
                if k == 0 and later(b, 2):
                    act.wait_ge(s_b, (b - 1) * STEPS)
                act.activation(Qt[par][:, 2 * k:2 * k + 2].rearrange("p n (g s) -> p n g s", g=G),
                               q_land[:].rearrange("p g (n s) -> p n g s", n=HEADS)[:, 2 * k:2 * k + 2],
                               ACT.Copy).then_inc(s_q_relaid, 1)

            def copy_o(b, g):
                act.wait_ge(s_pv, b * QUADS + 4 * g + 4)
                if g >= 2 or later(b):
                    act.wait_ge(s_o_stored[g % 2], (2 * b + g // 2) * 4 * DMA)
                act.activation(o_sb[:, g % 2], pv_bank[:], ACT.Copy).then_inc(s_o, 1)

            def stage(b, par):
                for r in range(QUADS):
                    if r < LAG and has(b, 1, NB):
                        exps(b - 1, r + QUADS - LAG)
                    if r >= LAG and has(b, 0, NB - 1):
                        exps(b, r - LAG)
                    if r <= LAG and (r + QUADS - LAG) % 4 == 0 and has(b, 1, NB):
                        copy_o(b - 1, (r + QUADS - LAG) // 4 - 1)
                    if r == LAG + 4 and has(b, 0, NB - 1):
                        copy_o(b, 0)
                    for q, what, db, g in misc_uses(5):
                        if q == r and what in ("x_turn", "q", "k", "v", "max_rows"):
                            if has(b, max(0, 5 - db), NB - 1 + 5 - db):
                                evacuate(what, b + (db - 5), g)
                    if LAG <= r and has(b, 0, NB - 2):
                        relay_q(b + 1, 1 - par, r - LAG)
                    if r == 0 and has(b, 0, NB - 1):
                        relay_q(b, par, QUADS - LAG)

            for what in ("x_turn", "q", "k", "v"):
                evacuate(what, 0)
            for k in range(QUADS - LAG):
                relay_q(0, 0, k)
            over_stages(act, stage)

            def f_piece(b, par, e):
                if e == 2:
                    act.wait_ge(s_f_full, 4 * b + 1)
                    act.activation(h2T[par], misc[:], ACT.Identity, bias=mod[:, 3, bass.ds(b, 1)],
                                   scale=mod[:, 4, bass.ds(b, 1)]).then_inc(s_f_read, 1)
                if e == 4:
                    act.wait_ge(s_gap, b + 1)
                    if later(b):
                        act.wait_ge(s_score, 2 * b)
                    act.activation(top_tanh[:], top_gap[:], ACT.Tanh, scale=0.5).then_inc(s_tanh, 1)
                if e == 5:
                    act.wait_ge(s_f_full, 4 * b + 3)
                    act.activation(w_rows[par][:], misc[:, 0:P], ACT.Copy).then_inc(s_f_read, 1)

            def expert(b, par, e):
                for c in range(HC):
                    u = (b * E + e) * HC + c
                    act.wait_ge(s_up, u + 1)
                    if e or later(b):
                        act.wait_ge(s_hid, u - 1)
                    act.activation(gate_act[:, c], up_bank[2 * c][:], ACT.Silu, bias=b1_sb[:, c, e:e + 1])\
                        .then_inc(s_act, 1)

            def f_batch(b, par, ahead):
                for e in range(E):
                    expert(b, par, e)
                    if ahead:
                        f_piece(b + 1, 1 - par, e)

            for e in range(E):
                f_piece(0, 0, e)
            f_batch(0, 0, True)
            f_batch(1, 1, True)
            with act.Fori(1, NB // 2 - 1, 1) as i:
                f_batch(2 * i, 0, True)
                f_batch(2 * i + 1, 1, True)
            f_batch(NB - 2, 0, True)
            f_batch(NB - 1, 1, False)

        @block.tensor
        def _(pe):
            pe.wait_ge(s_w, 6 * DMA)
            pe.wait_ge(s_const, N_CONST)
            pe.wait_ge(s_c_silu, 1)
            for j in range(6):
                ins = pe.matmul(misc[:, j * NB:(j + 1) * NB], wmod_sb[:, j], c_silu[:], start=True, stop=True)
            ins.then_inc(s_mod_mm, 1)
            pe.wait_ge(s_mod, 1)
            pe.transpose(misc[0:NB, 0:D], mod[:, 5], ident[:]).then_inc(s_gb_mm, 1)
            pe.wait_ge(s_gb, 1)

            def fill(what, b, g=0):
                n = misc_index(what, b, g)
                if what != "x_turn" or later(b):
                    n = n if isinstance(n, int) else pe.to_reg(n)
                    parts_ready = 4 * b + g + 1
                    if what == "max_rows" and not isinstance(b, int):
                        parts_ready = pe.to_reg(parts_ready)
                    wait_apart(pe, s_misc_read, n)
                if what == "x_turn":
                    pe.wait_ge(s_x_norm, b + 1)
                    for t in range(TT):
                        ins = pe.transpose(misc[:, P * t:P * t + P], x_norm[:, t], ident[:])
                if what in ("q", "k"):
                    w = wq_sb if what == "q" else wk_sb
                    ins = pe.matmul(misc[:], w[:], hT[:], start=True, stop=True)
                if what == "v":
                    for t in range(TT):
                        ins = pe.matmul(misc[:, P * t:P * t + P], hT[:, P * t:P * t + P], wv_sb[:],
                                        start=True, stop=True)
                if what == "max_rows":
                    pe.wait_ge(s_split_max[3], parts_ready)
                    ins = pe.transpose(misc_bf[0:PARTS * 16, 0:P], max_parts[:].rearrange("p i n -> p (i n)"),
                                       ident_bf[:])
                if what == "mean":
                    pe.wait_ge(s_y_mv, b + 1)
                    ins = pe.matmul(misc[:, 0:1], mean_mat[:], y_mv[:, 0:1], start=True, stop=True)
                if what == "var":
                    pe.wait_ge(s_y_sq, b + 1)
                    ins = pe.matmul(misc[:, 0:1], mean_mat[:], y_sq[:], start=True, stop=True)
                if what == "z_turn":
                    pe.wait_ge(s_z, b + 1)
                    for t in range(TT):
                        ins = pe.transpose(misc[:, P * t:P * t + P], z[:, P * t:P * t + P], ident[:])
                ins.then_inc(s_misc_full, 1)

            def pass_a(b, par, r, h):
                n, c = 4 * (r // 4) + h, r % 4
                m = b * STEPS + 4 * r + h
                if r % 4 == 0 and h == 0:
                    pe.wait_ge(s_q_relaid, 8 * b + r // 2 + 2)
                    pe.wait_ge(s_k_relaid, 4 * b + r // 4 + 1)
                s = 4 * r + h
                if s >= 3:
                    pe.wait_ge(s_max, m - 2)
                elif s == 0 and later(b):
                    pe.wait_ge(s_max, m)
                pe.matmul(score_a[s % 3][:], Qt[par][:, n, P * c:P * c + P], Kt[par][:, n],
                          start=True, stop=True).then_inc(s_a, 1)

            def pass_b(b, par, j, h):
                n, c = 4 * (j // 4) + h, j % 4
                m = b * STEPS + 4 * j + h
                if c == 0 and h == 0:
                    pe.wait_ge(s_max_moved, (4 * b + j // 4 + 1) * PARTS * DMA)
                s = 4 * j + h
                if s >= 3:
                    pe.wait_ge(s_exp, m - 2)
                elif s == 0 and later(b):
                    pe.wait_ge(s_exp, m)
                pe.matmul(score_b[s % 3][:], Kt[par][:, n, P * c:P * c + P], Qt[par][:, n],
                          start=True, stop=True).then_inc(s_b, 1)

            def values(b, par, j):
                g, c = j // 4, j % 4
                pe.wait_ge(s_exp, b * STEPS + 4 * j + 4)
                if j == 0:
                    pe.wait_ge(s_v_relaid, b + 1)
                if c == 0 and (g or later(b)):
                    pe.wait_ge(s_o, 4 * b + g)
                for h in range(4):
                    ins = pe.matmul(pv_bank[32 * h:32 * h + 2 * DK, :], Vt[:, par, 4 * (4 * g + h) + c], probs[:, 4 * (j % 2) + h],
                                    start=(c == 0), stop=(c == 3), tile_position=(0, 32 * h))
                ins.then_inc(s_pv, 1)

            def stage(b, par):
                for r in range(QUADS):
                    for h in range(4):
                        if has(b, 0, NB - 1):
                            pass_a(b, par, r, h)
                        if r < LAG and has(b, 1, NB):
                            pass_b(b - 1, 1 - par, r + QUADS - LAG, h)
                        if r >= LAG and has(b, 0, NB - 1):
                            pass_b(b, par, r - LAG, h)
                    if r <= LAG and has(b, 1, NB):
                        values(b - 1, 1 - par, r + QUADS - LAG - 1)
                    if r > LAG and has(b, 0, NB - 1):
                        values(b, par, r - LAG - 1)
                    for q, what, db, g in misc_uses(5):
                        if q == r and has(b, max(0, 5 - db), NB - 1 + 5 - db):
                            fill(what, b + (db - 5), g)

            for what in ("x_turn", "q", "k", "v"):
                fill(what, 0)
            over_stages(pe, stage)

            def f_piece(b, par, e):
                if e == 2:
                    if later(b):
                        pe.wait_ge(s_f_read, 4 * b)
                    pe.wait_ge(s_f_norm, b + 1)
                    for t in range(TT):
                        ins = pe.transpose(misc[:, P * t:P * t + P], f_norm[:, t], ident[:])
                    ins.then_inc(s_f_full, 1)
                if e == 3:
                    pe.wait_ge(s_f_read, 4 * b + 1)
                    for t in range(TT):
                        ins = pe.matmul(misc[:, E * t:E * t + E], h2T[par][:, P * t:P * t + P], gw_sb[:],
                                        start=True, stop=True)
                    ins.then_inc(s_f_full, 1)
                if e == 5:
                    pe.wait_ge(s_f_read, 4 * b + 2)
                    pe.wait_ge(s_wd, b + 1)
                    pe.transpose(misc[:, 0:P], w_dense[par][:].rearrange("p t e -> p (t e)"), ident[:])\
                        .then_inc(s_f_full, 1)
                if e == 6:
                    pe.wait_ge(s_f_read, 4 * b + 3)
                    for t in range(TT):
                        ins = pe.matmul(misc[:, P * t:P * t + P], w_rows[par][:], b3_sb[:, t],
                                        start=True, stop=True)
                    ins.then_inc(s_f_full, 1)

            def expert(b, par, e):
                for c in range(HC):
                    u = (b * E + e) * HC + c
                    if e or later(b):
                        pe.wait_ge(s_hid, u - 1)
                    pe.matmul(up_bank[2 * c][:], w1_sb[:, e, P * c:P * c + P], h2T[par], start=True, stop=True)
                    pe.matmul(up_bank[2 * c + 1][:], w2_sb[:, e, P * c:P * c + P], h2T[par],
                              start=True, stop=True).then_inc(s_up, 1)

            def down(b, par, e):
                w = b * E + e
                pe.wait_ge(s_hid, HC * (w + 1))
                if e >= 2 or later(b):
                    pe.wait_ge(s_acc, w - 1)
                for t in range(TT):
                    for c in range(HC):
                        ins = pe.matmul(down_bank[e % 2][:, P * t:P * t + P],
                                        hidden[HC * (e % 2) + c][:, P * t:P * t + P], w3_sb[:, e, c],
                                        start=(c == 0), stop=(c == HC - 1))
                ins.then_inc(s_down, 1)

            def f_batch(b, par, ahead):
                for e in range(E):
                    expert(b, par, e)
                    if e:
                        down(b, par, e - 1)
                    if ahead:
                        f_piece(b + 1, 1 - par, e)
                down(b, par, E - 1)

            pe.wait_ge(s_expert_w, (4 + HC + TT) * DMA)
            pe.wait_ge(s_max, NB * STEPS)
            pe.wait_ge(s_exp, NB * STEPS)
            pe.wait_ge(s_misc_read, len(MISC))
            for e in range(E):
                f_piece(0, 0, e)
            f_batch(0, 0, True)
            f_batch(1, 1, True)
            with pe.Fori(1, NB // 2 - 1, 1) as i:
                f_batch(2 * i, 0, True)
                f_batch(2 * i + 1, 1, True)
            f_batch(NB - 2, 0, True)
            f_batch(NB - 1, 1, False)


def kernel(**inputs):
    import concourse.bacc as _bacc
    from concourse.bass_utils import run_bass_kernel_spmd as _run

    nc = _bacc.Bacc("TRN2", target_bir_lowering=False, num_devices=1)
    a = {n: np.asarray(v) for n, v in inputs.items()}
    wv = a["L0_attn_Wv"].reshape(4, 4, DK, D).transpose(1, 0, 2, 3).reshape(D, D)
    laid = {
        "x": a["L0_attn_x"], "wqT": a["L0_attn_Wq"].T, "wkT": a["L0_attn_Wk"].T, "wvT": wv.T,
        "w1": a["L0_ffn_w1"], "b1T": a["L0_ffn_b1"].T, "w2": a["L0_ffn_w2"], "b2T": a["L0_ffn_b2"].T,
        "w3": a["L0_ffn_w3"], "b3": a["L0_ffn_b3"], "gate_w": a["L0_ffn_gate_w"],
        "cT": a["L0_c"].T, "wmod": a["L0_wmod"],
    }
    laid = {f"in_{n}": np.ascontiguousarray(v) for n, v in laid.items()}
    args = {n[3:]: nc.dram_tensor(n, v.shape, F32, kind="ExternalInput").ap() for n, v in laid.items()}
    args["out"] = nc.dram_tensor("out", (NB, S, D), F32, kind="ExternalOutput").ap()
    build(nc, **args)
    return _run(nc, [laid], core_ids=[0]).results[0]["out"]
```

```python
from contextlib import ExitStack

import numpy as np
import concourse.bass as bass
from concourse import mybir

F32 = mybir.dt.float32
BF16 = mybir.dt.bfloat16
F32R = mybir.dt.float32r
U32 = mybir.dt.uint32
I32 = mybir.dt.int32
ALU = mybir.AluOpType
ACT = mybir.ActivationFunctionType
AX_X = mybir.AxisListType.X

P = 128
NB, S, D = 16, 512, 128
HEADS, DK = 16, 8
G = D // DK
TOK = S // HEADS
PARTS = 3
ROWS = PARTS * PARTS * DK
MROW = 96
QUADS = 16
STEPS = 4 * QUADS
LAG = 9
TT = S // P
E, HID = 8, 256
HC = HID // P
EPS = 1e-5
TWO_ONES = 0x3F803F80
DMA = 16


def misc_uses(b):
    uses = [
        (1, "max_rows", b - 1, 3), (2, "x_turn", b + 1, 0), (3, "q", b + 1, 0), (4, "mean", b - 2, 0),
        (5, "max_rows", b, 0), (6, "k", b + 1, 0), (7, "v", b + 1, 0), (8, "var", b - 2, 0),
        (9, "max_rows", b, 1), (12, "z_turn", b - 2, 0), (13, "max_rows", b, 2),
    ]
    return [u for u in uses if 0 <= u[2] < NB]


def misc_table():
    order = [("x_turn", 0, 0), ("q", 0, 0), ("k", 0, 0), ("v", 0, 0)]
    for b in range(NB + 2):
        order += [u[1:] for u in misc_uses(b)]
    return {u: n for n, u in enumerate(order)}


MISC = misc_table()
MISC_PER_STAGE = len(misc_uses(5))


def misc_index(what, b, g=0):
    if isinstance(b, int):
        return MISC[(what, b, g)]
    return (b - 5) * MISC_PER_STAGE + MISC[(what, 5, g)]


def build(nc, x, wqT, wkT, wvT, w1, b1T, w2, b2T, w3, b3, gate_w, cT, wmod, out):
    ctx = ExitStack()
    with ctx:
        def sb(name, shape, dt=F32):
            return ctx.enter_context(nc.sbuf_tensor(name, shape, dt))

        def sem(name):
            return ctx.enter_context(nc.semaphore(name))

        def dram(name, shape, dt=F32):
            return nc.dram_tensor(name, shape, dt, kind="Internal").ap()

        q_dram = dram("q_dram", [PARTS, DK, HEADS, G, TOK], BF16)
        k_dram = dram("k_dram", [PARTS, DK, HEADS, G, TOK], BF16)
        v_dram = dram("v_dram", [S, D])
        h_dram = dram("h_dram", [NB, D, S])
        o_dram = dram("o_dram", [2, DK + 1, G, S])
        inv_dram = dram("inv_dram", [2, G, S])
        x2_dram = dram("x2_dram", [NB, S, D])
        gb_dram = dram("gb_dram", [NB, D])

        ident = sb("ident", [P, P])
        ident_bf = sb("ident_bf", [P, P], BF16)
        mean_mat = sb("mean_mat", [P, P])
        neg_half = sb("neg_half", [P, TT])
        iota8 = sb("iota8", [P, E])
        wq_sb = sb("wq_sb", [P, D])
        wk_sb = sb("wk_sb", [P, D])
        wv_sb = sb("wv_sb", [P, D])
        w1_sb = sb("w1_sb", [P, E, HID])
        w2_sb = sb("w2_sb", [P, E, HID])
        w3_sb = sb("w3_sb", [P, E, HC, D])
        b1_sb = sb("b1_sb", [P, HC, E])
        b2_sb = sb("b2_sb", [P, HC, E])
        b3_sb = sb("b3_sb", [P, TT, D])
        gw_sb = sb("gw_sb", [P, E])
        wmod_sb = sb("wmod_sb", [P, 6, D])
        c_sb = sb("c_sb", [P, NB])
        c_silu = sb("c_silu", [P, NB])
        mod = sb("mod", [P, 6, NB])
        mod_abs = sb("mod_abs", [P, 2, NB])
        mod_sign = sb("mod_sign", [P, 2, NB])
        gb_rows = sb("gb_rows", [NB, D])

        v_land = sb("v_land", [P, HEADS * 4, DK])
        Vt = sb("Vt", [P, 2, HEADS * 4, 2 * DK])
        probs = sb("probs", [P, 8, S])
        x_in = sb("x_in", [P, TT, D])
        x_stats = sb("x_stats", [P, TT, 6])
        x_mv = sb("x_mv", [P, TT, 2])
        x_ve = sb("x_ve", [P, TT])
        x_rstd = sb("x_rstd", [P, TT])
        x_shift = sb("x_shift", [P, TT])
        x_norm = sb("x_norm", [P, TT, D])
        hT = sb("hT", [P, S])
        q_f = sb("q_f", [P, S])
        k_f = sb("k_f", [P, S])
        v_f = sb("v_f", [P, TT, D])
        q_rest = sb("q_rest", [P, S])
        k_rest = sb("k_rest", [P, S])
        q_parts = sb("q_parts", [P, PARTS, S], BF16)
        k_parts = sb("k_parts", [P, PARTS, S], BF16)
        neg_max = sb("neg_max", [P, 2, 16])
        max_rest = sb("max_rest", [P, 16])
        max_parts = sb("max_parts", [P, PARTS, 16], BF16)
        max_rows = sb("max_rows", [PARTS * 16, P], BF16)
        o_sb = sb("o_sb", [P, 2, S])
        num = sb("num", [P, S])
        den = sb("den", [P, G * S // P])
        inv = sb("inv", [P, G * S // P])
        h_back = sb("h_back", [P, S])
        x_back = sb("x_back", [P, TT, D])
        den_inv = sb("den_inv", [P, S])
        attn = sb("attn", [P, S])
        y = sb("y", [P, S])
        y_stats = sb("y_stats", [P, 6])
        y_mv = sb("y_mv", [P, 2])
        y_mean = sb("y_mean", [P, 1])
        y_dev = sb("y_dev", [P, 1])
        y_dev2 = sb("y_dev2", [P, 1])
        y_sq = sb("y_sq", [P, 1])
        y_ve = sb("y_ve", [P, 1])
        y_rstd = sb("y_rstd", [P, 1])
        y_scale = sb("y_scale", [P, 1])
        y_shift = sb("y_shift", [P, 1])
        z = sb("z", [P, S])
        x2_out = sb("x2_out", [P, TT, D])
        gb_all = sb("gb_all", [P, 2, D])
        f_stats = sb("f_stats", [P, TT, 6])
        f_mv = sb("f_mv", [P, TT, 2])
        f_ve = sb("f_ve", [P, TT])
        f_rstd = sb("f_rstd", [P, TT])
        f_shift = sb("f_shift", [P, TT])
        logits = sb("logits", [P, TT, E])
        top = sb("top", [P, TT, 8])
        top_at = sb("top_at", [P, TT, 8], U32)
        top_at_f = sb("top_at_f", [P, TT, 2])
        top_gap = sb("top_gap", [P, TT])
        top_tanh = sb("top_tanh", [P, TT])
        score = sb("score", [P, 2, TT])
        pick = sb("pick", [P, 2, TT, E])
        w_dense = [sb(f"w_dense{i}", [P, TT, 32]) for i in range(2)]
        w_rows = [sb(f"w_rows{i}", [P, P]) for i in range(2)]

        w1_parts = sb("w1_parts", [P, 2, E, HID], F32R)
        w2_parts = sb("w2_parts", [P, 2, E, HID], F32R)
        with ExitStack() as attention:
            def sb_attention(name, shape):
                return attention.enter_context(nc.sbuf_tensor(name, shape, BF16))

            Qt0 = sb_attention("Qt0", [P, HEADS, S])
            Kt0 = sb_attention("Kt0", [P, HEADS, S])
            Qt = [Qt0, sb_attention("Qt1", [P, HEADS, S])]
            Kt = [Kt0, sb_attention("Kt1", [P, HEADS, S])]
        hidden = [sb(f"hidden{i}", [P, S])[:] for i in range(4)]
        gate_act = sb("gate_act", [P, HC, S])
        acc = sb("acc", [P, 2, TT, D])
        x2 = sb("x2", [P, 2, TT, D])
        h2T = [sb(f"h2T{i}", [P, S])[:] for i in range(2)]
        f_norm = sb("f_norm", [P, TT, D])
        h_parts = [[sb(f"h_part{i}{j}", [P, S], F32R)[:] for j in range(2)] for i in range(2)]
        y_out = sb("y_out", [P, 2, TT, D])

        bank = [ctx.enter_context(nc.psum_tensor(f"bank{i}", [P, S], F32)) for i in range(8)]
        score_a = bank[0:3]
        score_b = bank[3:6]
        pv_bank = bank[6]
        misc = bank[7]
        misc_bf = misc[:].bitcast(BF16)

        def end_bank(b):
            return pv_bank if isinstance(b, int) and b == NB - 1 else misc

        def front_bank(b):
            return score_a[0] if isinstance(b, int) and b == 0 else misc

        up_bank = bank[0:4]
        down_bank = bank[4:6]

        s_w = sem("s_w")
        s_expert_w = sem("s_expert_w")
        s_const = sem("s_const")
        s_clear = sem("s_clear")
        s_max_clear = sem("s_max_clear")
        s_clear_odd = sem("s_clear_odd")
        s_c_silu = sem("s_c_silu")
        s_mod_mm = sem("s_mod_mm")
        s_mod_chain = sem("s_mod_chain")
        s_mod = sem("s_mod")
        s_gb_mm = sem("s_gb_mm")
        s_gb = sem("s_gb")
        s_gb_dram = sem("s_gb_dram")
        s_misc_full = sem("s_misc_full")
        s_misc_read = sem("s_misc_read")
        s_x_in = sem("s_x_in")
        s_x_stats = sem("s_x_stats")
        s_x_mv = sem("s_x_mv")
        s_x_ve = sem("s_x_ve")
        s_x_rstd = sem("s_x_rstd")
        s_x_shift = sem("s_x_shift")
        s_x_norm = sem("s_x_norm")
        s_h_stored = sem("s_h_stored")
        s_split_q = [sem(f"s_split_q{i}") for i in range(4)]
        s_split_k = [sem(f"s_split_k{i}") for i in range(4)]
        s_q_stored = sem("s_q_stored")
        s_k_stored = sem("s_k_stored")
        s_v_stored = sem("s_v_stored")
        s_q_landed = sem("s_q_landed")
        s_k_landed = sem("s_k_landed")
        s_v_relaid = sem("s_v_relaid")
        s_v_loaded = sem("s_v_loaded")
        s_a = sem("s_a")
        s_max = sem("s_max")
        s_split_max = [sem(f"s_split_max{i}") for i in range(4)]
        s_max_moved = sem("s_max_moved")
        s_b = sem("s_b")
        s_exp = sem("s_exp")
        s_pv = sem("s_pv")
        s_o = sem("s_o")
        s_o_stored = [sem(f"s_o_stored{i}") for i in range(2)]
        s_back = sem("s_back")
        s_x_back = sem("s_x_back")
        s_den = sem("s_den")
        s_inv = sem("s_inv")
        s_inv_stored = sem("s_inv_stored")
        s_attn = sem("s_attn")
        s_y = sem("s_y")
        s_y_stats = sem("s_y_stats")
        s_y_mv = sem("s_y_mv")
        s_y_dev = sem("s_y_dev")
        s_y_dev2 = sem("s_y_dev2")
        s_y_sq = sem("s_y_sq")
        s_y_rstd = sem("s_y_rstd")
        s_y_scale = sem("s_y_scale")
        s_y_shift = sem("s_y_shift")
        s_z = sem("s_z")
        s_x2_stored = sem("s_x2_stored")
        s_w_first = sem("s_w_first")
        s_w_rest = sem("s_w_rest")
        s_h_rest = sem("s_h_rest")
        s_x2 = [sem(f"s_x2_{i}") for i in range(2)]
        s_f_stats = sem("s_f_stats")
        s_f_mv = sem("s_f_mv")
        s_f_ve = sem("s_f_ve")
        s_f_rstd = sem("s_f_rstd")
        s_f_shift = sem("s_f_shift")
        s_f_norm = sem("s_f_norm")
        s_f_full = sem("s_f_full")
        s_f_read = sem("s_f_read")
        s_top = sem("s_top")
        s_top_at = sem("s_top_at")
        s_gap = sem("s_gap")
        s_tanh = sem("s_tanh")
        s_score = sem("s_score")
        s_pick = sem("s_pick")
        s_wd = sem("s_wd")
        s_up = sem("s_up")
        s_act = sem("s_act")
        s_hid = sem("s_hid")
        s_down = sem("s_down")
        s_acc = sem("s_acc")
        s_scaled = sem("s_scaled")
        s_fin = sem("s_fin")
        s_out = [sem(f"s_out{i}") for i in range(2)]

        block = ctx.enter_context(nc.Block())

        def over_stages(eng, stage):
            stage(0, 0)
            stage(1, 1)
            with eng.Fori(1, NB // 2 - 1, 1) as i:
                stage(2 * i, 0)
                stage(2 * i + 1, 1)
            for b in range(NB - 2, NB + 1):
                stage(b, b % 2)

        def b_is(b, n):
            return isinstance(b, int) and b == n

        def has(b, first, last):
            return not isinstance(b, int) or first <= b <= last

        def later(b, n=1):
            return not isinstance(b, int) or b >= n

        N_CONST = 11

        def wait_apart(eng, semaphore, value):
            if isinstance(value, bass.RuntimeValue):
                value = eng.to_reg(value)
            eng.wait_ge(s_const, N_CONST)
            eng.wait_ge(semaphore, value)

        def split(eng, src, rest, parts, done, k):
            eng.tensor_copy(parts[:, 0], src).then_inc(done[0], 1)
            eng.wait_ge(done[0], k + 1)
            eng.tensor_tensor(rest, src, parts[:, 0], ALU.subtract).then_inc(done[1], 1)
            wait_apart(eng, done[1], k + 1)
            eng.tensor_copy(parts[:, 1], rest).then_inc(done[2], 1)
            eng.wait_ge(done[2], k + 1)
            eng.tensor_tensor(parts[:, 2], rest, parts[:, 1], ALU.subtract).then_inc(done[3], 1)

        def rows(operand, first, count):
            return operand[first:first + count].rearrange("p n q -> p (n q)").bitcast(I32)

        def set_rows(eng, par, done, between=lambda: None):
            eng.memset(rows(Kt[par], 64, P - 64), 0).then_inc(done, 1)
            between()
            eng.wait_ge(done, 1)
            eng.memset(rows(Kt[par], MROW, PARTS), TWO_ONES).then_inc(done, 1)
            eng.wait_ge(done, 2)
            eng.memset(rows(Qt[par], 64, P - 64), 0).then_inc(done, 1)

        @block.sync
        def _(sp):
            for dst, src in (
                (wmod_sb[:].rearrange("p j c -> p (j c)"), wmod), (c_sb[:], cT),
                (wq_sb[:], wqT), (wk_sb[:], wkT), (wv_sb[:], wvT), (gw_sb[:], gate_w),
            ):
                sp.dma_start(dst, src).then_inc(s_w, DMA)

            def x_load(b):
                if later(b):
                    wait_apart(sp, s_x_norm, TT * b)
                sp.dma_start(x_in[:], x[b].rearrange("(t p) c -> p t c", p=P)).then_inc(s_x_in, DMA)

            def front_store(b, what):
                if what == "x_turn":
                    wait_apart(sp, s_misc_read, misc_index("x_turn", b) + 1)
                    sp.dma_start(h_dram[b], hT[:]).then_inc(s_h_stored, DMA)
                if what == "q":
                    sp.wait_ge(s_split_q[3], b + 1)
                    for i in range(PARTS):
                        sp.dma_start(q_dram[i].rearrange("d n g s -> g d n s"),
                                     q_parts[:, i].rearrange("c (n s) -> c n s", s=TOK)).then_inc(s_q_stored, DMA)
                if what == "k":
                    sp.wait_ge(s_split_k[3], b + 1)
                    for i in range(PARTS):
                        sp.dma_start(k_dram[i].rearrange("d n g s -> g d n s"),
                                     k_parts[:, i].rearrange("c (n s) -> c n s", s=TOK)).then_inc(s_k_stored, DMA)
                if what == "v":
                    sp.wait_ge(s_misc_read, misc_index("v", b) + 1)
                    sp.dma_start(v_dram.rearrange("(t p) c -> p t c", p=P), v_f[:]).then_inc(s_v_stored, DMA)

            def q_load(b, par):
                if later(b, 2):
                    wait_apart(sp, s_b, (b - 1) * STEPS)
                sp.wait_ge(s_q_stored, (b + 1) * PARTS * DMA)
                for i in range(PARTS):
                    row = i * PARTS * DK
                    sp.dma_start(Qt[par][row:row + PARTS * DK].rearrange("r n q -> r (n q)"),
                                 q_dram[i:i + 1].rearrange("i d n g s -> i d (n g s)")
                                 .broadcast_to([PARTS, DK, HEADS * S])).then_inc(s_q_landed, DMA)

            def k_load(b, par):
                sp.wait_ge(s_k_stored, (b + 1) * PARTS * DMA)
                for i in range(PARTS):
                    row = i * PARTS * DK
                    sp.dma_start(Kt[par][row:row + PARTS * DK].rearrange("r n q -> r (n q)"),
                                 k_dram.rearrange("j d n g s -> (j d) (n g s)")).then_inc(s_k_landed, DMA)

            def v_load(b):
                if later(b):
                    wait_apart(sp, s_v_relaid, b)
                sp.wait_ge(s_v_stored, (b + 1) * DMA)
                for g in range(4):
                    sp.dma_start(
                        v_land[32 * g:32 * g + TOK].rearrange("p (n i) d -> p n (i d)", n=HEADS),
                        v_dram.rearrange("(n p) (g w) -> g p n w", p=TOK, g=4)[g]).then_inc(s_v_loaded, DMA)

            def max_move(b, par, g):
                sp.wait_ge(s_misc_read, misc_index("max_rows", b, g) + 1)
                for i in range(PARTS):
                    sp.dma_start(Qt[par][MROW + i:MROW + i + 1, 4 * g:4 * g + 4]
                                 .rearrange("o h (c p) -> o (h c) p", p=P), max_rows[16 * i:16 * i + 16])\
                        .then_inc(s_max_moved, DMA)

            def o_store(b, par, g):
                sp.wait_ge(s_o, 4 * b + g + 1)
                for h in range(4):
                    sp.dma_start(
                        o_dram[par, :, :, P * g + TOK * h:P * g + TOK * h + TOK],
                        o_sb[32 * h:32 * h + DK + 1, g % 2, :].rearrange("d (g s) -> d g s", s=TOK))\
                        .then_inc(s_o_stored[g % 2], DMA)

            def back_load(b, par):
                for i in range(2):
                    sp.wait_ge(s_o_stored[i], (b + 1) * 8 * DMA)
                if later(b):
                    sp.wait_ge(s_y, b)
                sp.dma_start(den[:], o_dram[par, DK].rearrange("g s -> (g s)").rearrange("(p i) -> p i", p=P))\
                    .then_inc(s_den, DMA)
                sp.dma_start(num[:], o_dram[par, 0:DK].rearrange("d g s -> g d s")).then_inc(s_back, DMA)
                wait_apart(sp, s_h_stored, (b + 1) * DMA)
                sp.dma_start(h_back[:], h_dram[b]).then_inc(s_back, DMA)

            def inv_store(b, par):
                sp.wait_ge(s_inv, b + 1)
                sp.dma_start(inv_dram[par].rearrange("g s -> (g s)").rearrange("(p i) -> p i", p=P), inv[:])\
                    .then_inc(s_inv_stored, DMA)

            def inv_load(b, par):
                sp.wait_ge(s_inv_stored, (b + 1) * DMA)
                sp.dma_start(den_inv[:], inv_dram[par].rearrange("(g o) s -> g o s", o=1).broadcast_to([G, DK, S]))\
                    .then_inc(s_back, DMA)

            def x_back_load(b):
                if later(b):
                    wait_apart(sp, s_misc_read, misc_index("z_turn", b - 1) + 1)
                sp.dma_start(x_back[:], x[b].rearrange("(t p) c -> p t c", p=P)).then_inc(s_x_back, DMA)

            def x2_store(b):
                wait_apart(sp, s_misc_read, misc_index("z_turn", b) + 1)
                sp.dma_start(x2_dram[b].rearrange("(t p) c -> p t c", p=P), x2_out[:]).then_inc(s_x2_stored, DMA)

            def f_load(b, par):
                if later(b, 2):
                    wait_apart(sp, s_fin, b - 1)
                sp.dma_start(x2[:, par], x2_dram[b].rearrange("(t p) c -> p t c", p=P)).then_inc(s_x2[par], DMA)
                sp.dma_start(gb_all[:, par], gb_dram[bass.ds(b, 1)].broadcast_to([P, D])).then_inc(s_x2[par], DMA)

            def stage(b, par):
                if b_is(b, NB):
                    sp.wait_ge(s_b, (NB - 1) * STEPS)
                    sp.wait_ge(s_x2_stored, 2 * DMA)
                    sp.wait_ge(s_gb_dram, DMA)
                    f_load(0, 0)
                    f_load(1, 1)
                if has(b, 1, NB):
                    max_move(b - 1, 1 - par, 3)
                    o_store(b - 1, 1 - par, 1)
                if has(b, 0, NB - 2):
                    front_store(b + 1, "x_turn")
                if has(b, 0, NB - 3):
                    x_load(b + 2)
                if has(b, 0, NB - 1):
                    max_move(b, par, 0)
                if has(b, 2, NB + 1):
                    x_back_load(b - 2)
                if has(b, 1, NB):
                    o_store(b - 1, 1 - par, 2)
                if has(b, 0, NB - 2):
                    front_store(b + 1, "q")
                    q_load(b + 1, 1 - par)
                    front_store(b + 1, "v")
                if has(b, 0, NB - 1):
                    max_move(b, par, 1)
                if has(b, 0, NB - 2):
                    front_store(b + 1, "k")
                    k_load(b + 1, 1 - par)
                if has(b, 1, NB):
                    o_store(b - 1, 1 - par, 3)
                if has(b, 0, NB - 2):
                    v_load(b + 1)
                if has(b, 1, NB):
                    back_load(b - 1, 1 - par)
                if has(b, 0, NB - 1):
                    max_move(b, par, 2)
                if has(b, 2, NB + 1):
                    x2_store(b - 2)
                if has(b, 0, NB - 1):
                    o_store(b, par, 0)
                if has(b, 1, NB):
                    inv_store(b - 1, 1 - par)
                    inv_load(b - 1, 1 - par)

            x_load(0)
            for dst, src in (
                (w1_sb[:], w1.rearrange("e i h -> i e h")), (w2_sb[:], w2.rearrange("e i h -> i e h")),
                (b1_sb[:], b1T.rearrange("(c p) e -> p c e", p=P)),
                (b2_sb[:], b2T.rearrange("(c p) e -> p c e", p=P)),
            ):
                sp.dma_start(dst, src).then_inc(s_expert_w, DMA)
            for c in range(HC):
                sp.dma_start(w3_sb[:, :, c], w3[:, c * P:(c + 1) * P].rearrange("e p d -> p e d")).then_inc(s_expert_w, DMA)
            sp.wait_ge(s_const, N_CONST)
            for t in range(TT):
                sp.dma_start(b3_sb[32 * t:32 * t + E, t], b3).then_inc(s_expert_w, DMA)
            front_store(0, "x_turn")
            x_load(1)
            sp.wait_ge(s_clear, 4)
            sp.wait_ge(s_clear_odd, 3)
            front_store(0, "q")
            front_store(0, "k")
            q_load(0, 0)
            k_load(0, 0)
            front_store(0, "v")
            v_load(0)
            sp.wait_ge(s_gb, 1)
            sp.dma_start(gb_dram, gb_rows[:]).then_inc(s_gb_dram, DMA)
            over_stages(sp, stage)

            def f_store(b, par):
                wait_apart(sp, s_fin, b + 1)
                sp.dma_start(out[b].rearrange("(t p) c -> p t c", p=P), y_out[:, par]).then_inc(s_out[par], DMA)

            x_back_load(NB - 1)
            x2_store(NB - 1)
            sp.wait_ge(s_x2_stored, NB * DMA)
            with sp.Fori(0, NB // 2 - 1, 1) as i:
                for par in range(2):
                    f_store(2 * i + par, par)
                    f_load(2 * i + par + 2, par)
            for b in (NB - 2, NB - 1):
                f_store(b, b % 2)
            for par in range(2):
                sp.wait_ge(s_out[par], NB // 2 * DMA)

        @block.gpsimd
        def _(pool):
            pool.memset(ident[:], 0.0).then_inc(s_const, 1)
            pool.memset(ident_bf[:], 0.0).then_inc(s_const, 1)
            pool.memset(mean_mat[:], 1.0 / P).then_inc(s_const, 1)
            pool.memset(neg_half[:], -0.5).then_inc(s_const, 1)
            pool.iota(iota8[:], [[1, E]], base=0, channel_multiplier=0,
                      allow_small_or_imprecise_dtypes=True).then_inc(s_const, 1)
            pool.memset(Vt[:], 1.0).then_inc(s_const, 1)
            pool.memset(b3_sb[:], 0.0).then_inc(s_const, 1)
            pool.wait_ge(s_const, 7)
            for m in (ident, ident_bf):
                pool.affine_select(out=m[:], in_=m[:], compare_op=ALU.not_equal, fill=1.0, base=0,
                                   pattern=[[-1, P]], channel_multiplier=1).then_inc(s_const, 1)
            for i in range(2):
                pool.memset(w_dense[i][:], 0.0).then_inc(s_const, 1)

            def split_q(b):
                wait_apart(pool, s_misc_read, misc_index("q", b) + 1)
                if later(b):
                    wait_apart(pool, s_q_stored, b * PARTS * DMA)
                split(pool, q_f[:], q_rest[:], q_parts, s_split_q, b)

            def split_k(b):
                wait_apart(pool, s_misc_read, misc_index("k", b) + 1)
                if later(b):
                    wait_apart(pool, s_k_stored, b * PARTS * DMA)
                split(pool, k_f[:], k_rest[:], k_parts, s_split_k, b)

            def split_max(b, g):
                gg = 4 * b + g
                pool.wait_ge(s_max, (gg + 1) * 16)
                if g or later(b):
                    pb, pg = (b, g - 1) if g else (b - 1, 3)
                    wait_apart(pool, s_misc_full, misc_index("max_rows", pb, pg) + 1)
                split(pool, neg_max[:, g % 2], max_rest[:], max_parts, s_split_max, gg)

            def relay_v(b, par):
                wait_apart(pool, s_v_loaded, (b + 1) * 4 * DMA)
                if later(b, 2):
                    wait_apart(pool, s_pv, (b - 1) * QUADS)
                pool.tensor_copy(Vt[:, par, :, 0:DK], v_land[:]).then_inc(s_v_relaid, 1)

            def clear_max(b, par):
                wait_apart(pool, s_split_k[3], b + 1)
                if later(b, 3):
                    pool.wait_ge(s_y_rstd, b - 2)
                wait_apart(pool, s_b, (b - 1) * STEPS)
                pool.memset(rows(Qt[par], MROW, PARTS), 0).then_inc(s_max_clear, 1)
                wait_apart(pool, s_max_clear, b - 1)

            def x_power(b):
                pool.wait_ge(s_x_ve, b + 1)
                pool.tensor_tensor(x_rstd[:], x_ve[:], neg_half[:], ALU.pow).then_inc(s_x_rstd, 1)

            def y_power(b):
                pool.wait_ge(s_misc_read, misc_index("var", b) + 1)
                pool.tensor_tensor(y_rstd[:], y_ve[:], neg_half[:, 0:1], ALU.pow).then_inc(s_y_rstd, 1)

            def add_h(b):
                pool.wait_ge(s_back, (b + 1) * 3 * DMA)
                pool.tensor_tensor(attn[:], num[:], den_inv[:], ALU.mult).then_inc(s_attn, 1)
                pool.wait_ge(s_attn, b + 1)
                if later(b):
                    pool.wait_ge(s_z, b)
                pool.tensor_tensor(y[:], attn[:], h_back[:], ALU.add).then_inc(s_y, 1)

            def f_power(b):
                pool.wait_ge(s_f_ve, b + 1)
                pool.tensor_tensor(f_rstd[:], f_ve[:], neg_half[:], ALU.pow).then_inc(s_f_rstd, 1)

            def stage(b, par):
                if has(b, 1, NB):
                    split_max(b - 1, 3)
                if b_is(b, NB):
                    f_power(0)
                if has(b, 0, NB - 2):
                    x_power(b + 1)
                if has(b, 2, NB + 1):
                    add_h(b - 2)
                if has(b, 0, NB - 1):
                    split_max(b, 0)
                if has(b, 0, NB - 2):
                    split_q(b + 1)
                if has(b, 0, NB - 1):
                    relay_v(b, par)
                    split_max(b, 1)
                if has(b, 0, NB - 2):
                    split_k(b + 1)
                if has(b, 2, NB + 1):
                    y_power(b - 2)
                if has(b, 1, NB - 2):
                    clear_max(b + 1, 1 - par)
                if has(b, 0, NB - 1):
                    split_max(b, 2)

            x_power(0)
            pool.wait_ge(s_x_rstd, 1)
            set_rows(pool, 1, s_clear_odd)
            pool.wait_ge(s_clear_odd, 3)
            pool.wait_ge(s_split_k[3], 1)
            pool.wait_ge(s_split_q[3], 1)
            over_stages(pool, stage)

            add_h(NB - 1)
            f_power(1)
            y_power(NB - 1)

            def finish(b, par):
                pool.wait_ge(s_acc, (b + 1) * E)
                if later(b, 2):
                    wait_apart(pool, s_out[par], (b - par) * (DMA // 2))
                pool.tensor_tensor(y_out[:, par], acc[:, par],
                                   gb_all[:, par].unsqueeze(1).broadcast_to([P, TT, D]), ALU.mult)\
                    .then_inc(s_scaled, 1)
                pool.wait_ge(s_scaled, b + 1)
                pool.tensor_tensor(y_out[:, par], y_out[:, par], x2[:, par], ALU.add).then_inc(s_fin, 1)

            for b in range(2):
                finish(b, b)
                f_power(b + 2)
            with pool.Fori(1, NB // 2 - 1, 1) as i:
                for par in range(2):
                    finish(2 * i + par, par)
                    f_power(2 * i + par + 2)
            for b in (NB - 2, NB - 1):
                finish(b, b % 2)

        @block.vector
        def _(dve):
            link_count = [0]

            def link(ins):
                link_count[0] += 1
                ins.then_inc(s_mod_chain, 1)
                dve.wait_ge(s_mod_chain, link_count[0])

            def modulation():
                dve.wait_ge(s_mod_mm, 1)
                link(dve.tensor_copy(mod[:].rearrange("p j b -> p (j b)"), misc[:, 0:6 * NB]))
                gates = mod[:].rearrange("p (k j) b -> p k j b", j=3)[:, :, 2]
                scales = mod[:].rearrange("p (k j) b -> p k j b", j=3)[:, :, 1]
                link(dve.tensor_scalar(scales, scales, 1.0, None, ALU.add))
                link(dve.tensor_scalar(mod_sign[:], gates, 0.0, 2.0, ALU.is_ge, ALU.mult))
                link(dve.tensor_scalar(mod_sign[:], mod_sign[:], 1.0, None, ALU.subtract))
                link(dve.tensor_tensor(mod_abs[:], mod_sign[:], gates, ALU.mult))
                link(dve.tensor_scalar(mod_abs[:], mod_abs[:], 0.25, None, ALU.max))
                dve.tensor_tensor(gates, mod_sign[:], mod_abs[:], ALU.mult).then_inc(s_mod, 1)
                dve.wait_ge(s_gb_mm, 1)
                dve.tensor_copy(gb_rows[:], misc[0:NB, 0:D]).then_inc(s_gb, 1)

            def aggregate(st, mv, ve, k, s_st, s_mv, s_ve):
                wait_apart(dve, s_st, TT * (k + 1))
                for t in range(TT):
                    dve.bn_aggr(mv[:, t], st[:, t]).then_inc(s_mv, 1)
                dve.wait_ge(s_mv, TT * (k + 1))
                dve.tensor_scalar(ve[:], mv[:, :, 1], EPS, None, ALU.add).then_inc(s_ve, 1)

            def front_stats(b, tiles):
                if tiles[0] == 0:
                    dve.wait_ge(s_x_in, (b + 1) * DMA)
                for t in tiles:
                    dve.bn_stats(x_stats[:, t], x_in[:, t]).then_inc(s_x_stats, 1)

            def front_shift(b):
                dve.wait_ge(s_x_rstd, b + 1)
                if later(b):
                    dve.wait_ge(s_x_norm, TT * b)
                dve.scalar_tensor_tensor(x_shift[:], x_mv[:, :, 0], -1.0, x_rstd[:], ALU.mult, ALU.mult)\
                    .then_inc(s_x_shift, 1)

            def maxima(b, par, r):
                g, c = r // 4, r % 4
                if c == 0 and (g >= 2 or later(b)):
                    dve.wait_ge(s_split_max[3], 4 * b + g - 1)
                for h in range(4):
                    dve.wait_ge(s_a, b * STEPS + 4 * r + h + 1)
                    dve.tensor_reduce(neg_max[:, g % 2, 4 * h + c:4 * h + c + 1], score_a[(4 * r + h + par) % 3][:],
                                      AX_X, ALU.max, negate=True).then_inc(s_max, 1)

            def end_inv(b):
                dve.wait_ge(s_den, (b + 1) * DMA)
                if later(b):
                    dve.wait_ge(s_inv_stored, b * DMA)
                dve.reciprocal(inv[:], den[:]).then_inc(s_inv, 1)

            def end_stats(b):
                dve.wait_ge(s_y, b + 1)
                dve.bn_stats(y_stats[:], y[:]).then_inc(s_y_stats, 1)
                wait_apart(dve, s_y_stats, b + 1)
                dve.bn_aggr(y_mv[:], y_stats[:]).then_inc(s_y_mv, 1)

            def end_dev(b):
                dve.wait_ge(s_misc_full, misc_index("mean", b) + 1)
                dve.tensor_copy(y_mean[:], end_bank(b)[:, 0:1]).then_inc(s_misc_read, 1)
                dve.wait_ge(s_misc_read, misc_index("mean", b) + 1)
                dve.tensor_tensor(y_dev[:], y_mv[:, 0:1], y_mean[:], ALU.subtract).then_inc(s_y_dev, 1)
                dve.wait_ge(s_y_dev, b + 1)
                dve.tensor_tensor(y_dev2[:], y_dev[:], y_dev[:], ALU.mult).then_inc(s_y_dev2, 1)
                dve.wait_ge(s_y_dev2, b + 1)
                dve.tensor_tensor(y_sq[:], y_dev2[:], y_mv[:, 1:2], ALU.add).then_inc(s_y_sq, 1)

            def end_var(b):
                dve.wait_ge(s_misc_full, misc_index("var", b) + 1)
                dve.tensor_scalar(y_ve[:], end_bank(b)[:, 0:1], EPS, None, ALU.add).then_inc(s_misc_read, 1)

            def end_shift(b):
                dve.wait_ge(s_y_rstd, b + 1)
                if later(b):
                    dve.wait_ge(s_z, b)
                dve.tensor_tensor(y_scale[:], mod[:, 2, bass.ds(b, 1)], y_rstd[:], ALU.mult).then_inc(s_y_scale, 1)
                dve.wait_ge(s_y_scale, b + 1)
                dve.scalar_tensor_tensor(y_shift[:], y_mean[:], -1.0, y_scale[:], ALU.mult, ALU.mult)\
                    .then_inc(s_y_shift, 1)

            def end_x2(b):
                dve.wait_ge(s_misc_full, misc_index("z_turn", b) + 1)
                if later(b):
                    dve.wait_ge(s_x2_stored, b * DMA)
                dve.wait_ge(s_x_back, (b + 1) * DMA)
                dve.tensor_tensor(x2_out[:].rearrange("p t c -> p (t c)"), end_bank(b)[:],
                                  x_back[:].rearrange("p t c -> p (t c)"), ALU.add).then_inc(s_misc_read, 1)

            def f_piece(b, par, e):
                if e == 1:
                    dve.wait_ge(s_x2[par], (b - par + 2) * DMA)
                    for t in range(TT):
                        dve.bn_stats(f_stats[:, t], x2[:, par, t]).then_inc(s_f_stats, 1)
                    aggregate(f_stats, f_mv, f_ve, b, s_f_stats, s_f_mv, s_f_ve)
                if e == 2:
                    dve.wait_ge(s_f_rstd, b + 1)
                    if later(b):
                        dve.wait_ge(s_f_full, 4 * b - 3)
                    dve.scalar_tensor_tensor(f_shift[:], f_mv[:, :, 0], -1.0, f_rstd[:], ALU.mult, ALU.mult)\
                        .then_inc(s_f_shift, 1)
                    dve.wait_ge(s_f_shift, b + 1)
                    for t in range(TT):
                        dve.tensor_scalar(f_norm[:, t], x2[:, par, t], f_rstd[:, t:t + 1], f_shift[:, t:t + 1],
                                          ALU.mult, ALU.add).then_inc(s_f_norm, 1)
                if e == 4:
                    wait_apart(dve, s_f_read, 4 * b + 1)
                    dve.tensor_tensor(h_parts[par][1], h2T[par], h_parts[par][0].bitcast(F32), ALU.subtract)\
                        .then_inc(s_h_rest, 1)
                    dve.wait_ge(s_f_full, 4 * b + 2)
                    dve.tensor_copy(logits[:].rearrange("p t e -> p (t e)"), front_bank(b)[:, 0:TT * E])\
                        .then_inc(s_f_read, 1)
                    wait_apart(dve, s_f_read, 4 * b + 2)
                    for t in range(TT):
                        dve.max(top[:, t], logits[:, t]).then_inc(s_top, 1)
                    dve.wait_ge(s_top, TT * (b + 1))
                    if later(b):
                        dve.wait_ge(s_tanh, b)
                    dve.tensor_tensor(top_gap[:], top[:, :, 0], top[:, :, 1], ALU.subtract).then_inc(s_gap, 1)
                    for t in range(TT):
                        dve.max_index(top_at[:, t], top[:, t], logits[:, t]).then_inc(s_top_at, 1)
                if e == 5:
                    dve.wait_ge(s_top_at, (TT + 1) * b + TT)
                    dve.tensor_copy(top_at_f[:], top_at[:, :, 0:2]).then_inc(s_top_at, 1)
                    dve.wait_ge(s_tanh, b + 1)
                    for k in range(2):
                        dve.tensor_scalar(score[:, k], top_tanh[:], 0.5 - k, 0.5, ALU.mult, ALU.add)\
                            .then_inc(s_score, 1)
                    dve.wait_ge(s_top_at, (TT + 1) * (b + 1))
                    dve.wait_ge(s_score, 2 * (b + 1))
                    for k in range(2):
                        for t in range(TT):
                            dve.tensor_scalar(pick[:, k, t], iota8[:], top_at_f[:, t, k:k + 1],
                                              score[:, k, t:t + 1], ALU.is_equal, ALU.mult).then_inc(s_pick, 1)
                    dve.wait_ge(s_pick, 2 * TT * (b + 1))
                    dve.tensor_tensor(w_dense[par][:, :, 0:E], pick[:, 0], pick[:, 1], ALU.add).then_inc(s_wd, 1)
                if e == 7:
                    if later(b, 2):
                        dve.wait_ge(s_scaled, b - 1)
                    dve.wait_ge(s_f_full, 4 * b + 4)
                    dve.tensor_copy(acc[:, par].rearrange("p t c -> p (t c)"), front_bank(b)[:]).then_inc(s_f_read, 1)

            def stage(b, par):
                for r in range(QUADS):
                    if has(b, 0, NB - 2):
                        if r == 0:
                            aggregate(x_stats, x_mv, x_ve, b + 1, s_x_stats, s_x_mv, s_x_ve)
                        if r == 1:
                            front_shift(b + 1)
                    if r in (13, 15) and has(b, 0, NB - 3):
                        front_stats(b + 2, range(r - 13, r - 11))
                    if has(b, 2, NB + 1):
                        if r == 4:
                            end_stats(b - 2)
                        if r == 5:
                            end_dev(b - 2)
                        if r == 9:
                            end_var(b - 2)
                        if r == 11:
                            end_shift(b - 2)
                        if r == 13:
                            end_x2(b - 2)
                    if has(b, 0, NB - 1):
                        maxima(b, par, r)
                    if r == 15 and has(b, 1, NB - 1):
                        end_inv(b - 1)
                    if b_is(b, NB) and 1 <= r <= E:
                        f_piece(0, 0, r - 1)

            def first_front():
                modulation()
                front_stats(0, range(TT))
                aggregate(x_stats, x_mv, x_ve, 0, s_x_stats, s_x_mv, s_x_ve)
                front_shift(0)

            set_rows(dve, 0, s_clear, between=first_front)
            dve.memset(pv_bank[:], 0.0).then_inc(s_clear, 1)
            dve.wait_ge(s_misc_read, misc_index("q", 0) + 1)
            split(dve, q_f[:], q_rest[:], q_parts, s_split_q, 0)
            dve.wait_ge(s_misc_read, misc_index("k", 0) + 1)
            split(dve, k_f[:], k_rest[:], k_parts, s_split_k, 0)
            front_stats(1, range(TT))
            for k, (w, parts) in enumerate(((w1_sb, w1_parts), (w2_sb, w2_parts))):
                dve.wait_ge(s_w_first, k + 1)
                dve.tensor_tensor(parts[:, 1], w[:], parts[:, 0].bitcast(F32), ALU.subtract).then_inc(s_w_rest, 1)
            over_stages(dve, stage)

            def expert(b, par, e):
                for c in range(HC):
                    u = (b * E + e) * HC + c
                    slot = HC * (e % 2) + c
                    dve.wait_ge(s_act, u + 1)
                    if e >= 2 or later(b):
                        dve.wait_ge(s_down, b * E + e - 1)
                    dve.scalar_tensor_tensor(hidden[slot], up_bank[2 * c + 1][:], b2_sb[:, c, e:e + 1],
                                             gate_act[:, c], ALU.add, ALU.mult).then_inc(s_hid, 1)

            def add_expert(b, par, e):
                w = b * E + e
                dve.wait_ge(s_down, w + 1)
                if e or later(b):
                    dve.wait_ge(s_acc, w)
                if e == 0:
                    dve.wait_ge(s_f_read, 4 * b + 4)
                for t in range(TT):
                    ins = dve.scalar_tensor_tensor(acc[:, par, t], down_bank[e % 2][:, P * t:P * t + P],
                                                   w_dense[par][:, t, e:e + 1], acc[:, par, t],
                                                   ALU.mult, ALU.add)
                ins.then_inc(s_acc, 1)

            def end_piece(e):
                steps = {0: end_inv, 2: end_stats, 4: end_dev, 6: end_var, 7: end_shift, E: end_x2}
                if e in steps:
                    steps[e](NB - 1)

            def f_batch(b, par, ahead):
                for e in range(E):
                    expert(b, par, e)
                    if e:
                        add_expert(b, par, e - 1)
                    if b_is(b, 0):
                        end_piece(e)
                    if ahead:
                        f_piece(b + 1, 1 - par, e)
                add_expert(b, par, E - 1)
                if b_is(b, 0):
                    end_piece(E)

            f_batch(0, 0, True)
            f_batch(1, 1, True)
            with dve.Fori(1, NB // 2 - 1, 1) as i:
                f_batch(2 * i, 0, True)
                f_batch(2 * i + 1, 1, True)
            f_batch(NB - 2, 0, True)
            f_batch(NB - 1, 1, False)

        @block.scalar
        def _(act):
            act.wait_ge(s_w, 6 * DMA)
            act.activation(c_silu[:], c_sb[:], ACT.Silu).then_inc(s_c_silu, 1)
            act.wait_ge(s_mod, 1)

            def evacuate(what, b, g=0):
                act.wait_ge(s_misc_full, misc_index(what, b, g) + 1)
                if what == "x_turn":
                    if later(b):
                        act.wait_ge(s_h_stored, b * DMA)
                    ins = act.activation(hT[:], misc[:], ACT.Identity, bias=mod[:, 0, bass.ds(b, 1)],
                                         scale=mod[:, 1, bass.ds(b, 1)])
                if what == "q":
                    if later(b):
                        act.wait_ge(s_split_q[1], b)
                    ins = act.activation(q_f[:], misc[:], ACT.Copy)
                if what == "k":
                    if later(b):
                        act.wait_ge(s_split_k[1], b)
                    ins = act.activation(k_f[:], misc[:], ACT.Copy)
                if what == "v":
                    if later(b):
                        act.wait_ge(s_v_stored, b * DMA)
                    ins = act.activation(v_f[:].rearrange("p t c -> p (t c)"), misc[:], ACT.Copy)
                if what == "max_rows":
                    if g or later(b):
                        act.wait_ge(s_max_moved, (4 * b + g) * PARTS * DMA)
                    ins = act.activation(max_rows[:], misc_bf[0:PARTS * 16, 0:P], ACT.Copy)
                ins.then_inc(s_misc_read, 1)

            def front_norm(b, tiles):
                if tiles[0] == 0:
                    act.wait_ge(s_x_shift, b + 1)
                    if later(b):
                        act.wait_ge(s_misc_full, misc_index("x_turn", b - 1) + 1)
                for t in tiles:
                    act.activation(x_norm[:, t], x_in[:, t], ACT.Identity, bias=x_shift[:, t:t + 1],
                                   scale=x_rstd[:, t:t + 1]).then_inc(s_x_norm, 1)

            def end_z(b):
                act.wait_ge(s_y_shift, b + 1)
                if later(b):
                    act.wait_ge(s_misc_full, misc_index("z_turn", b - 1) + 1)
                act.activation(z[:], y[:], ACT.Identity, bias=y_shift[:], scale=y_scale[:]).then_inc(s_z, 1)

            def exps(b, par, j, halfway=lambda: None):
                if j >= 2 or later(b):
                    act.wait_ge(s_pv, b * QUADS + j - 1)
                for h in range(4):
                    n = b * STEPS + 4 * j + h
                    act.wait_ge(s_b, n + 1)
                    act.activation(probs[:, 4 * (j % 2) + h], score_b[(4 * j + h + par) % 3][:], ACT.Exp).then_inc(s_exp, 1)
                    if h == 1:
                        halfway()

            def copy_o(b, g):
                act.wait_ge(s_pv, b * QUADS + 4 * g + 4)
                if g >= 2 or later(b):
                    act.wait_ge(s_o_stored[g % 2], (2 * b + g // 2) * 4 * DMA)
                act.activation(o_sb[:, g % 2], pv_bank[:], ACT.Copy).then_inc(s_o, 1)

            def f_piece(b, par, e):
                if e == 3:
                    act.wait_ge(s_f_full, 4 * b + 1)
                    act.activation(h2T[par], front_bank(b)[:], ACT.Identity, bias=mod[:, 3, bass.ds(b, 1)],
                                   scale=mod[:, 4, bass.ds(b, 1)])
                    act.activation(h_parts[par][0], front_bank(b)[:], ACT.Identity, bias=mod[:, 3, bass.ds(b, 1)],
                                   scale=mod[:, 4, bass.ds(b, 1)]).then_inc(s_f_read, 1)
                if e == 5:
                    act.wait_ge(s_gap, b + 1)
                    if later(b):
                        act.wait_ge(s_score, 2 * b)
                    act.activation(top_tanh[:], top_gap[:], ACT.Tanh, scale=0.5).then_inc(s_tanh, 1)
                if e == 6:
                    act.wait_ge(s_f_full, 4 * b + 3)
                    act.activation(w_rows[par][:], front_bank(b)[:, 0:P], ACT.Copy).then_inc(s_f_read, 1)

            def stage(b, par):
                for r in range(QUADS):
                    if r == 2 and has(b, 1, NB - 2):
                        exps(b - 1, 1 - par, r + QUADS - LAG, halfway=lambda: front_norm(b + 1, (2, 3)))
                    elif r == 2 and has(b, 0, 0):
                        front_norm(b + 1, (2, 3))
                    elif r < LAG and has(b, 1, NB):
                        exps(b - 1, 1 - par, r + QUADS - LAG)
                    elif r >= LAG and has(b, 0, NB - 1):
                        exps(b, par, r - LAG)
                    if r == 1 and has(b, 0, NB - 2):
                        front_norm(b + 1, (0, 1))
                    if r == 11 and has(b, 2, NB):
                        end_z(b - 2)
                    if r <= LAG and (r + QUADS - LAG) % 4 == 0 and has(b, 1, NB):
                        copy_o(b - 1, (r + QUADS - LAG) // 4 - 1)
                    if r == LAG + 4 and has(b, 0, NB - 1):
                        copy_o(b, 0)
                    for q, what, db, g in misc_uses(5):
                        if q == r and what in ("x_turn", "q", "k", "v", "max_rows"):
                            if has(b, max(0, 5 - db), NB - 1 + 5 - db):
                                evacuate(what, b + (db - 5), g)
                    if b_is(b, NB) and 1 <= r <= E:
                        f_piece(0, 0, r - 1)

            front_norm(0, range(TT))
            for what in ("x_turn", "q", "k", "v"):
                evacuate(what, 0)
            act.wait_ge(s_expert_w, (4 + HC + TT) * DMA)
            for w, parts in ((w1_sb, w1_parts), (w2_sb, w2_parts)):
                act.activation(parts[:, 0], w[:], ACT.Copy).then_inc(s_w_first, 1)
            over_stages(act, stage)

            def expert(b, par, e):
                for c in range(HC):
                    u = (b * E + e) * HC + c
                    act.wait_ge(s_up, u + 1)
                    if e or later(b):
                        act.wait_ge(s_hid, u - 1)
                    act.activation(gate_act[:, c], up_bank[2 * c][:], ACT.Silu, bias=b1_sb[:, c, e:e + 1])\
                        .then_inc(s_act, 1)

            def f_batch(b, par, ahead):
                for e in range(E):
                    expert(b, par, e)
                    if ahead:
                        f_piece(b + 1, 1 - par, e)
                if b_is(b, 0):
                    end_z(NB - 1)

            f_batch(0, 0, True)
            f_batch(1, 1, True)
            with act.Fori(1, NB // 2 - 1, 1) as i:
                f_batch(2 * i, 0, True)
                f_batch(2 * i + 1, 1, True)
            f_batch(NB - 2, 0, True)
            f_batch(NB - 1, 1, False)

        @block.tensor
        def _(pe):
            pe.wait_ge(s_w, 6 * DMA)
            pe.wait_ge(s_const, N_CONST)
            pe.wait_ge(s_c_silu, 1)
            for j in range(6):
                ins = pe.matmul(misc[:, j * NB:(j + 1) * NB], wmod_sb[:, j], c_silu[:], start=True, stop=True)
            ins.then_inc(s_mod_mm, 1)
            pe.wait_ge(s_mod, 1)
            pe.transpose(misc[0:NB, 0:D], mod[:, 5], ident[:]).then_inc(s_gb_mm, 1)
            pe.wait_ge(s_gb, 1)

            def fill(what, b, g=0):
                n = misc_index(what, b, g)
                if what != "x_turn" or later(b):
                    n = n if isinstance(n, int) else pe.to_reg(n)
                    parts_ready = 4 * b + g + 1
                    if what == "max_rows" and not isinstance(b, int):
                        parts_ready = pe.to_reg(parts_ready)
                    wait_apart(pe, s_misc_read, n)
                if what == "x_turn":
                    pe.wait_ge(s_x_norm, TT * (b + 1))
                    for t in range(TT):
                        ins = pe.transpose(misc[:, P * t:P * t + P], x_norm[:, t], ident[:])
                if what in ("q", "k"):
                    w = wq_sb if what == "q" else wk_sb
                    ins = pe.matmul(misc[:], w[:], hT[:], start=True, stop=True)
                if what == "v":
                    for t in range(TT):
                        ins = pe.matmul(misc[:, P * t:P * t + P], hT[:, P * t:P * t + P], wv_sb[:],
                                        start=True, stop=True)
                if what == "max_rows":
                    pe.wait_ge(s_split_max[3], parts_ready)
                    ins = pe.transpose(misc_bf[0:PARTS * 16, 0:P], max_parts[:].rearrange("p i n -> p (i n)"),
                                       ident_bf[:])
                if what == "mean":
                    pe.wait_ge(s_y_mv, b + 1)
                    ins = pe.matmul(end_bank(b)[:, 0:1], mean_mat[:], y_mv[:, 0:1], start=True, stop=True)
                if what == "var":
                    pe.wait_ge(s_y_sq, b + 1)
                    ins = pe.matmul(end_bank(b)[:, 0:1], mean_mat[:], y_sq[:], start=True, stop=True)
                if what == "z_turn":
                    pe.wait_ge(s_z, b + 1)
                    for t in range(TT):
                        ins = pe.transpose(end_bank(b)[:, P * t:P * t + P], z[:, P * t:P * t + P], ident[:])
                ins.then_inc(s_misc_full, 1)

            def steps_since(s, par):
                return 2 if par == 0 and s < 2 else 3

            def pass_a(b, par, r, h):
                n, c = 4 * (r // 4) + h, r % 4
                m = b * STEPS + 4 * r + h
                if r + h == 0:
                    if later(b, 2):
                        pe.wait_ge(s_max_clear, b - 1)
                    pe.wait_ge(s_q_landed, (b + 1) * PARTS * DMA)
                    pe.wait_ge(s_k_landed, (b + 1) * PARTS * DMA)
                s = 4 * r + h
                if s >= 3 or later(b):
                    pe.wait_ge(s_max, m - steps_since(s, par) + 1)
                pe.matmul(score_a[(s + par) % 3][:], Qt[par][:, n, P * c:P * c + P], Kt[par][:, n],
                          start=True, stop=True).then_inc(s_a, 1)

            def pass_b(b, par, j, h):
                n, c = 4 * (j // 4) + h, j % 4
                m = b * STEPS + 4 * j + h
                if c == 0 and h == 0:
                    pe.wait_ge(s_max_moved, (4 * b + j // 4 + 1) * PARTS * DMA)
                s = 4 * j + h
                if s >= 3 or later(b):
                    pe.wait_ge(s_exp, m - steps_since(s, par) + 1)
                pe.matmul(score_b[(s + par) % 3][:], Kt[par][:, n, P * c:P * c + P], Qt[par][:, n],
                          start=True, stop=True).then_inc(s_b, 1)

            def values(b, par, j):
                g, c = j // 4, j % 4
                pe.wait_ge(s_exp, b * STEPS + 4 * j + 4)
                if j == 0:
                    pe.wait_ge(s_v_relaid, b + 1)
                if c == 0 and (g or later(b)):
                    pe.wait_ge(s_o, 4 * b + g)
                for h in range(4):
                    ins = pe.matmul(pv_bank[32 * h:32 * h + 2 * DK, :], Vt[:, par, 4 * (4 * g + h) + c], probs[:, 4 * (j % 2) + h],
                                    start=(c == 0), stop=(c == 3), tile_position=(0, 32 * h))
                ins.then_inc(s_pv, 1)

            def f_piece(b, par, e):
                if e == 3:
                    if b_is(b, 0):
                        pe.wait_ge(s_max, NB * STEPS)
                    elif b_is(b, 1):
                        pe.wait_ge(s_misc_read, misc_index("mean", NB - 1))
                    else:
                        pe.wait_ge(s_f_read, 4 * b)
                    pe.wait_ge(s_f_norm, TT * (b + 1))
                    for t in range(TT):
                        ins = pe.transpose(front_bank(b)[:, P * t:P * t + P], f_norm[:, t], ident[:])
                    ins.then_inc(s_f_full, 1)
                if e == 4:
                    pe.wait_ge(s_f_read, 4 * b + 1)
                    for t in range(TT):
                        ins = pe.matmul(front_bank(b)[:, E * t:E * t + E], h2T[par][:, P * t:P * t + P], gw_sb[:],
                                        start=True, stop=True)
                    ins.then_inc(s_f_full, 1)
                if e == 6:
                    pe.wait_ge(s_f_read, 4 * b + 2)
                    pe.wait_ge(s_wd, b + 1)
                    pe.transpose(front_bank(b)[:, 0:P], w_dense[par][:].rearrange("p t e -> p (t e)"), ident[:])\
                        .then_inc(s_f_full, 1)
                if e == 7:
                    pe.wait_ge(s_f_read, 4 * b + 3)
                    for t in range(TT):
                        ins = pe.matmul(front_bank(b)[:, P * t:P * t + P], w_rows[par][:], b3_sb[:, t],
                                        start=True, stop=True)
                    ins.then_inc(s_f_full, 1)

            def stage(b, par):
                for r in range(QUADS):
                    for h in range(4):
                        if has(b, 0, NB - 1):
                            pass_a(b, par, r, h)
                        if r < LAG and has(b, 1, NB):
                            pass_b(b - 1, 1 - par, r + QUADS - LAG, h)
                        if r >= LAG and has(b, 0, NB - 1):
                            pass_b(b, par, r - LAG, h)
                    if r <= LAG and has(b, 1, NB):
                        values(b - 1, 1 - par, r + QUADS - LAG - 1)
                    if r > LAG and has(b, 0, NB - 1):
                        values(b, par, r - LAG - 1)
                    for q, what, db, g in misc_uses(5):
                        if q == r and has(b, max(0, 5 - db), NB - 1 + 5 - db):
                            fill(what, b + (db - 5), g)
                    if b_is(b, NB) and 1 <= r <= E:
                        f_piece(0, 0, r - 1)

            for what in ("x_turn", "q", "k", "v"):
                fill(what, 0)
            over_stages(pe, stage)

            def expert(b, par, e):
                if e == 0:
                    pe.wait_ge(s_h_rest, b + 1)
                for c in range(HC):
                    u = (b * E + e) * HC + c
                    if e or later(b):
                        pe.wait_ge(s_hid, u - 1)
                    for k, w in enumerate((w1_parts, w2_parts)):
                        for i, j in ((0, 0), (0, 1), (1, 0)):
                            ins = pe.matmul(up_bank[2 * c + k][:], w[:, i, e, P * c:P * c + P], h_parts[par][j],
                                            start=(i + j == 0), stop=(i == 1))
                    ins.then_inc(s_up, 1)

            def down(b, par, e):
                w = b * E + e
                pe.wait_ge(s_hid, HC * (w + 1))
                if e >= 2 or later(b):
                    pe.wait_ge(s_acc, w - 1)
                for t in range(TT):
                    for c in range(HC):
                        ins = pe.matmul(down_bank[e % 2][:, P * t:P * t + P],
                                        hidden[HC * (e % 2) + c][:, P * t:P * t + P], w3_sb[:, e, c],
                                        start=(c == 0), stop=(c == HC - 1))
                ins.then_inc(s_down, 1)

            def end_piece(e):
                if e == 3:
                    pe.wait_ge(s_o, 4 * NB)
                    fill("mean", NB - 1)
                if e == 5:
                    fill("var", NB - 1)
                if e == E:
                    fill("z_turn", NB - 1)

            def f_batch(b, par, ahead):
                for e in range(E):
                    expert(b, par, e)
                    if e:
                        down(b, par, e - 1)
                    if b_is(b, 0):
                        end_piece(e)
                    if ahead:
                        f_piece(b + 1, 1 - par, e)
                down(b, par, E - 1)
                if b_is(b, 0):
                    end_piece(E)

            pe.wait_ge(s_expert_w, (4 + HC + TT) * DMA)
            pe.wait_ge(s_w_rest, 2)
            pe.wait_ge(s_exp, NB * STEPS)
            pe.wait_ge(s_f_read, 4)
            f_batch(0, 0, True)
            f_batch(1, 1, True)
            with pe.Fori(1, NB // 2 - 1, 1) as i:
                f_batch(2 * i, 0, True)
                f_batch(2 * i + 1, 1, True)
            f_batch(NB - 2, 0, True)
            f_batch(NB - 1, 1, False)


def kernel(**inputs):
    import concourse.bacc as _bacc
    from concourse.bass_utils import run_bass_kernel_spmd as _run

    nc = _bacc.Bacc("TRN2", target_bir_lowering=False, num_devices=1)
    a = {n: np.asarray(v) for n, v in inputs.items()}
    wv = a["L0_attn_Wv"].reshape(4, 4, DK, D).transpose(1, 0, 2, 3).reshape(D, D)
    laid = {
        "x": a["L0_attn_x"], "wqT": a["L0_attn_Wq"].T, "wkT": a["L0_attn_Wk"].T, "wvT": wv.T,
        "w1": a["L0_ffn_w1"], "b1T": a["L0_ffn_b1"].T, "w2": a["L0_ffn_w2"], "b2T": a["L0_ffn_b2"].T,
        "w3": a["L0_ffn_w3"], "b3": a["L0_ffn_b3"], "gate_w": a["L0_ffn_gate_w"],
        "cT": a["L0_c"].T, "wmod": a["L0_wmod"],
    }
    laid = {f"in_{n}": np.ascontiguousarray(v) for n, v in laid.items()}
    args = {n[3:]: nc.dram_tensor(n, v.shape, F32, kind="ExternalInput").ap() for n, v in laid.items()}
    args["out"] = nc.dram_tensor("out", (NB, S, D), F32, kind="ExternalOutput").ap()
    build(nc, **args)
    return _run(nc, [laid], core_ids=[0]).results[0]["out"]
```
